# Optimizing a Trainium2 kernel written in Bass

```python
import numpy as np
import jax
import jax.numpy as jnp

def _softmax(x, axis=-1):
    return jax.nn.softmax(x, axis=axis)

def _gelu(x):
    return jax.nn.gelu(x, approximate=True)

def _silu(x):
    return jax.nn.silu(x)

def _sigmoid(x):
    return jax.nn.sigmoid(x)

def _layernorm(x, axis=-1, eps=1e-05):
    m = jnp.mean(x, axis=axis, keepdims=True)
    v = jnp.var(x, axis=axis, keepdims=True)
    return (x - m) / jnp.sqrt(v + eps)

def _scatter_add(tgt, idx, src, axis=0):
    return tgt.at[idx].add(src)

def _segment_sum(src, seg, n):
    return jax.ops.segment_sum(src, seg, n)
kernel_name = 'mk_seq_postln_d1_jaxref_r8_d15575'

def setup_inputs(seed: int=0):
    np.random.seed(seed)
    _w = jnp.asarray

    def _L0_attn_setup():
        import jax, jax.numpy as jnp
        import numpy as np
        HID, H, KV, D = (256, 16, 4, 128)
        ROPE_THETA = 10000.0
        GATE_NORM = 16.0

        def _rope_cos_sin(n, d, dtype=jnp.float32):
            inv_freq = 1.0 / ROPE_THETA ** (jnp.arange(0, d, 2, dtype=jnp.float32) / d)
            freqs = jnp.arange(n, dtype=jnp.float32)[:, None] * inv_freq[None, :]
            cos = jnp.cos(freqs).astype(dtype)[None, :, None, :]
            sin = jnp.sin(freqs).astype(dtype)[None, :, None, :]
            return (cos, sin)

        def _apply_rotary(x, cos, sin):
            x1, x2 = jnp.split(x, 2, axis=-1)
            return jnp.concatenate([x1 * cos - x2 * sin, x2 * cos + x1 * sin], axis=-1)

        def _forward(hidden_states, Wq, Wk, Wv, Wo):
            b, n, _ = hidden_states.shape
            groups = H // KV
            q = hidden_states @ Wq
            k = hidden_states @ Wk
            v = hidden_states @ Wv
            g = k
            q = q.reshape(b, n, H, D)
            k = k.reshape(b, n, KV, D)
            v = v.reshape(b, n, KV, D)
            g = g.reshape(b, n, KV, D)
            k = jnp.repeat(k, groups, axis=2)
            v = jnp.repeat(v, groups, axis=2)
            g = jnp.repeat(g, groups, axis=2)
            sq, sk, sv = (q, k, v)
            qs = jax.nn.softmax(q.astype(jnp.float32), axis=-1)
            ks = jax.nn.softmax(k.astype(jnp.float32), axis=-1)
            gl = jax.nn.log_sigmoid(g.astype(jnp.float32)) / GATE_NORM
            cos, sin = _rope_cos_sin(n, D)
            sq = _apply_rotary(sq, cos, sin)
            sk = _apply_rotary(sk, cos, sin)

            def step(S, inp):
                q_t, k_t, v_t, g_t = inp
                S = S * jnp.exp(g_t)[..., None] + k_t[..., None] * v_t[..., None, :]
                o_t = jnp.einsum('bhk,bhkv->bhv', q_t, S)
                return (S, o_t)
            xs = tuple((jnp.moveaxis(a, 1, 0) for a in (qs, ks, v, gl)))
            S0 = jnp.zeros((b, H, D, D), dtype=jnp.float32)
            _, o_gla = jax.lax.scan(step, S0, xs)
            o_gla = jnp.moveaxis(o_gla, 0, 1)
            scale = D ** (-0.5)
            scores = jnp.einsum('bqhd,bkhd->bhqk', sq, sk) * scale
            causal = jnp.tril(jnp.ones((n, n), dtype=bool))
            scores = jnp.where(causal[None, None], scores, jnp.finfo(scores.dtype).min)
            attn = jax.nn.softmax(scores, axis=-1)
            y = jnp.einsum('bhqk,bkhd->bqhd', attn, sv)
            o = 0.5 * y + 0.5 * o_gla
            o = o.reshape(b, n, H * D).astype(hidden_states.dtype)
            return o @ Wo
        key = jax.random.key(seed)
        k1, k2, k3, k4, k5 = jax.random.split(key, 5)
        s = 0.02
        return {'hidden_states': jax.random.normal(k1, (1, 256, HID), dtype=jnp.float32), 'Wq': jax.random.normal(k2, (HID, H * D), dtype=jnp.float32) * s, 'Wk': jax.random.normal(k3, (HID, KV * D), dtype=jnp.float32) * s, 'Wv': jax.random.normal(k4, (HID, KV * D), dtype=jnp.float32) * s, 'Wo': jax.random.normal(k5, (H * D, HID), dtype=jnp.float32) * s}
    _L0_attn_in = _L0_attn_setup()

    def _L0_ffn_setup():
        import jax, jax.numpy as jnp
        import numpy as np
        TOP_K = 2
        key = jax.random.key(seed)
        k1, k2, k3, k4, k5 = jax.random.split(key, 5)
        B, S, D = (1, 256, 256)
        E, F = (8, 176)
        scale = 0.02
        return {'hidden_states': jax.random.normal(k1, (B, S, D), dtype=jnp.float32), 'gate_w': jax.random.normal(k2, (E, D), dtype=jnp.float32) * scale, 'w_gate': jax.random.normal(k3, (E, D, F), dtype=jnp.float32) * scale, 'w_up': jax.random.normal(k4, (E, D, F), dtype=jnp.float32) * scale, 'w_down': jax.random.normal(k5, (E, F, D), dtype=jnp.float32) * scale}
    _L0_ffn_in = _L0_ffn_setup()
    _d = {'L0_attn_hidden_states': _L0_attn_in['hidden_states'], 'L0_attn_Wq': _L0_attn_in['Wq'], 'L0_attn_Wk': _L0_attn_in['Wk'], 'L0_attn_Wv': _L0_attn_in['Wv'], 'L0_attn_Wo': _L0_attn_in['Wo'], 'L0_ffn_gate_w': _L0_ffn_in['gate_w'], 'L0_ffn_w_gate': _L0_ffn_in['w_gate'], 'L0_ffn_w_up': _L0_ffn_in['w_up'], 'L0_ffn_w_down': _L0_ffn_in['w_down']}
    _x0 = _d['L0_attn_hidden_states']
    _d['L0_attn_hidden_states'] = jax.random.normal(jax.random.fold_in(jax.random.key(seed), 1), (4, 512, 256), dtype=_x0.dtype)
    del _x0
    return _d

def reference(L0_attn_hidden_states, L0_attn_Wq, L0_attn_Wk, L0_attn_Wv, L0_attn_Wo, L0_ffn_gate_w, L0_ffn_w_gate, L0_ffn_w_up, L0_ffn_w_down):

    def _L0_attn_ref(hidden_states, Wq, Wk, Wv, Wo):
        import jax, jax.numpy as jnp
        import numpy as np
        HID, H, KV, D = (256, 16, 4, 128)
        ROPE_THETA = 10000.0
        GATE_NORM = 16.0

        def _rope_cos_sin(n, d, dtype=jnp.float32):
            inv_freq = 1.0 / ROPE_THETA ** (jnp.arange(0, d, 2, dtype=jnp.float32) / d)
            freqs = jnp.arange(n, dtype=jnp.float32)[:, None] * inv_freq[None, :]
            cos = jnp.cos(freqs).astype(dtype)[None, :, None, :]
            sin = jnp.sin(freqs).astype(dtype)[None, :, None, :]
            return (cos, sin)

        def _apply_rotary(x, cos, sin):
            x1, x2 = jnp.split(x, 2, axis=-1)
            return jnp.concatenate([x1 * cos - x2 * sin, x2 * cos + x1 * sin], axis=-1)

        def _forward(hidden_states, Wq, Wk, Wv, Wo):
            b, n, _ = hidden_states.shape
            groups = H // KV
            q = hidden_states @ Wq
            k = hidden_states @ Wk
            v = hidden_states @ Wv
            g = k
            q = q.reshape(b, n, H, D)
            k = k.reshape(b, n, KV, D)
            v = v.reshape(b, n, KV, D)
            g = g.reshape(b, n, KV, D)
            k = jnp.repeat(k, groups, axis=2)
            v = jnp.repeat(v, groups, axis=2)
            g = jnp.repeat(g, groups, axis=2)
            sq, sk, sv = (q, k, v)
            qs = jax.nn.softmax(q.astype(jnp.float32), axis=-1)
            ks = jax.nn.softmax(k.astype(jnp.float32), axis=-1)
            gl = jax.nn.log_sigmoid(g.astype(jnp.float32)) / GATE_NORM
            cos, sin = _rope_cos_sin(n, D)
            sq = _apply_rotary(sq, cos, sin)
            sk = _apply_rotary(sk, cos, sin)

            def step(S, inp):
                q_t, k_t, v_t, g_t = inp
                S = S * jnp.exp(g_t)[..., None] + k_t[..., None] * v_t[..., None, :]
                o_t = jnp.einsum('bhk,bhkv->bhv', q_t, S)
                return (S, o_t)
            xs = tuple((jnp.moveaxis(a, 1, 0) for a in (qs, ks, v, gl)))
            S0 = jnp.zeros((b, H, D, D), dtype=jnp.float32)
            _, o_gla = jax.lax.scan(step, S0, xs)
            o_gla = jnp.moveaxis(o_gla, 0, 1)
            scale = D ** (-0.5)
            scores = jnp.einsum('bqhd,bkhd->bhqk', sq, sk) * scale
            causal = jnp.tril(jnp.ones((n, n), dtype=bool))
            scores = jnp.where(causal[None, None], scores, jnp.finfo(scores.dtype).min)
            attn = jax.nn.softmax(scores, axis=-1)
            y = jnp.einsum('bhqk,bkhd->bqhd', attn, sv)
            o = 0.5 * y + 0.5 * o_gla
            o = o.reshape(b, n, H * D).astype(hidden_states.dtype)
            return o @ Wo
        return _forward(hidden_states, Wq, Wk, Wv, Wo)

    def _L0_ffn_ref(hidden_states, gate_w, w_gate, w_up, w_down):
        import jax, jax.numpy as jnp
        import numpy as np
        TOP_K = 2
        B, S, D = hidden_states.shape
        T = B * S
        x = hidden_states.reshape(T, D)
        router_logits = jnp.einsum('td,ed->te', x, gate_w)
        routing_weights = jax.nn.softmax(router_logits, axis=-1)
        top_w, top_idx = jax.lax.top_k(routing_weights, TOP_K)
        comb = jnp.zeros((T, gate_w.shape[0]), dtype=routing_weights.dtype)
        comb = comb.at[jnp.arange(T)[:, None], top_idx].add(top_w)
        g = jnp.einsum('td,edf->etf', x, w_gate)
        u = jnp.einsum('td,edf->etf', x, w_up)
        y = jnp.einsum('etf,efd->etd', jax.nn.silu(g) * u, w_down)
        out = jnp.einsum('te,etd->td', comb, y)
        return out.reshape(B, S, D)
    x = L0_attn_hidden_states
    x = _layernorm(x + _L0_attn_ref(x, L0_attn_Wq, L0_attn_Wk, L0_attn_Wv, L0_attn_Wo), axis=-1)
    x = _layernorm(x + _L0_ffn_ref(x, L0_ffn_gate_w, L0_ffn_w_gate, L0_ffn_w_up, L0_ffn_w_down), axis=-1)
    return x

_drawn_inputs = setup_inputs


def setup_inputs(seed=0):
    import zlib

    import numpy as np

    out = dict(_drawn_inputs(seed))
    spreads = {}
    factors = {'L0_attn_Wq': 8.0,
     'L0_attn_Wk': 8.0,
     'L0_attn_Wv': 3.074,
     'L0_attn_Wo': 2.977,
     'L0_ffn_gate_w': 8.0,
     'L0_ffn_w_gate': 8.0,
     'L0_ffn_w_up': 8.0,
     'L0_ffn_w_down': 8.0}
    for name, (base, spread) in spreads.items():
        noise = np.random.default_rng([zlib.crc32(name.encode()), seed]).standard_normal(out[name].shape)
        drawn = base * np.exp(spread * noise) if base else spread * noise
        out[name] = jnp.asarray(drawn.astype(out[name].dtype))
    for name, factor in factors.items():
        out[name] = (out[name] * factor).astype(out[name].dtype)
    return out
```

```python
from contextlib import ExitStack

import concourse.bass as bass
from concourse import mybir

F32 = mybir.dt.float32
F32R = mybir.dt.float32r
BF16 = mybir.dt.bfloat16
ALU = mybir.AluOpType
ACT = mybir.ActivationFunctionType
AX_X = mybir.AxisListType.X

P128 = 128
B, N, HID = 4, 512, 256
H, KV, D = 16, 4, 128
GQ = H // KV
C = N // P128
NG = B * KV
NU = NG * C
KT2 = HID // P128
QKV = GQ * D + 2 * D
QK = GQ * D + D
GATE_NORM = 16.0
GCLAMP = 80.0 * GATE_NORM
EPS = 1e-5
E, F = 8, 176
FT = E * F // P128
TILES = B * N // P128
NGRP = B * N // 512
NEG = -1.0e30


def later(eng, sem, value):
    if isinstance(value, int) and value <= 0:
        return
    eng.wait_ge(sem, value)


def tri(c):
    return c * (c + 1) // 2


def layer_kernel(nc, x_rows, x_cols, wqkv, wo_in, wgu, wdn, gate, rope_cos, rope_sin, cmat, cmask, csel, out):
    with ExitStack() as ctx:
        def sb(name, shape, dt):
            return ctx.enter_context(nc.sbuf_tensor(name, shape, dt))

        def pb(name, shape):
            return ctx.enter_context(nc.psum_tensor(name, shape, F32))

        def sem(name):
            return ctx.enter_context(nc.semaphore(name))

        w_hi = sb("w_hi", [P128, KV * KT2 * QKV], F32R)
        w_lo = sb("w_lo", [P128, KV * KT2 * QKV], F32R)
        xT_hi = sb("xT_hi", [P128, KT2 * B * N], F32R)
        xT_lo = sb("xT_lo", [P128, KT2 * B * N], F32R)
        wo = sb("wo", [P128, H, HID], F32)
        acc = sb("acc", [P128, TILES, HID], F32)
        cos = sb("cos", [P128, C, D], F32)
        sin = sb("sin", [P128, C, D], F32)
        gate_hi = sb("gate_hi", [P128, KT2, P128], F32R)
        gate_lo = sb("gate_lo", [P128, KT2, P128], F32R)
        sel = sb("sel", [P128, FT, P128], F32R)
        cm = sb("cm", [P128, 3 * P128 + 2], F32)
        ident = cm[:, 0:128]
        keep = cm[:, 128:256]
        gmat = cm[:, 256:384]
        early, late = cm[:, 384:385], cm[:, 385:386]
        maskb = sb("maskb", [P128, 2, P128], BF16)
        tri8 = sb("tri8", [P128, E, E], F32)
        neghalf = sb("neghalf", [P128, C], F32)

        ring_hi = sb("ring_hi", [P128, C, KT2, P128], F32R)
        ring_lo = sb("ring_lo", [P128, C, KT2, P128], F32R)
        qkv = sb("qkv", [P128, C, QKV], F32)
        eqk = sb("eqk", [P128, 2, QK], F32)
        rt = sb("rt", [P128, 2, QK], F32)
        rp = sb("rp", [P128, 2, QK], F32)
        qd = sb("qd", [P128, 2, QK], F32)
        rqT = sb("rqT", [P128, GQ * P128], F32)
        KT = sb("KT", [P128, C * P128], F32)
        qdT = sb("qdT", [P128, 2, GQ * P128], F32)
        kdT = sb("kdT", [P128, P128], F32)
        pr = sb("pr", [P128, GQ, N], F32)
        wT = sb("wT", [P128, C, GQ * P128], F32)
        am = sb("am", [P128, GQ * P128], F32)
        oT = sb("oT", [P128, GQ * P128], F32)
        V = sb("V", [P128, C, D], F32)
        U = sb("U", [P128, D], F32)
        Ut = sb("Ut", [P128, D], F32)
        eg = sb("eg", [P128, 2, 2 * P128 + 2], F32)
        gc = sb("gc", [P128, P128 + 1], F32)
        gl = sb("gl", [P128, 2, D], F32)
        nabs = sb("nabs", [P128, D], F32)
        eabs = sb("eabs", [P128, D], F32)
        lnp = sb("lnp", [P128, D], F32)
        nmx = sb("nmx", [P128, GQ + 1], F32)
        se = sb("se", [P128, GQ + 1], F32)
        rse = sb("rse", [P128, 2, GQ + 1], F32)
        nm = sb("nm", [P128, GQ], F32)
        ls = sb("ls", [P128, GQ], F32)
        rl = sb("rl", [P128, GQ], F32)
        st = sb("st", [P128, 4, 6], F32)
        mv = sb("mv", [P128, 4, 2], F32)
        ve = sb("ve", [P128, 4], F32)
        rstd = sb("rstd", [P128, 4], F32)
        st2 = sb("st2", [P128, 4, 6], F32)
        mv2 = sb("mv2", [P128, 4, 2], F32)
        ve2 = sb("ve2", [P128, 4], F32)
        rstd2 = sb("rstd2", [P128, 4], F32)
        pad = sb("pad", [P128, 1], F32)
        lg = sb("lg", [P128, 4, E], F32)
        lx = sb("lx", [P128, 4, E], F32)
        pe_ = sb("pe_", [P128, 4, E], F32)
        rank = sb("rank", [P128, 4, E], F32)
        topm = sb("topm", [P128, 4, E], F32)
        comb = sb("comb", [P128, 4, E], F32)
        small = sb("small", [P128, 12], F32)
        rk1 = sb("rk1", [P128, 4 * E * E], F32)
        rk2 = sb("rk2", [P128, 4 * E * E], F32)

        prf = pr[:, :, :].rearrange("p a b -> p (a b)")
        wTf = wT[:, :, :].rearrange("p a b -> p (a b)")
        qkvf = qkv[:, :, :].rearrange("p a b -> p (a b)")
        eqkf = eqk[:, :, :].rearrange("p a b -> p (a b)")
        rtf = rt[:, :, :].rearrange("p a b -> p (a b)")
        rpf = rp[:, :, :].rearrange("p a b -> p (a b)")

        gu_hi = w_hi[:, 0:FT * KT2 * 2 * P128].rearrange("p (f k w c) -> p f k w c", f=FT, k=KT2, w=2)
        gu_lo = w_lo[:, 0:FT * KT2 * 2 * P128].rearrange("p (f k w c) -> p f k w c", f=FT, k=KT2, w=2)
        combT = w_hi[:, FT * KT2 * 2 * P128:FT * KT2 * 2 * P128 + 512]
        dn_hi = xT_hi[:, 0:FT * HID].rearrange("p (f n) -> p f n", f=FT)
        dn_lo = xT_lo[:, 0:FT * HID].rearrange("p (f n) -> p f n", f=FT)
        hT_hi = xT_hi[:, FT * HID:FT * HID + 1024].rearrange("p (a n) -> p a n", a=2)
        hT_lo = xT_lo[:, FT * HID:FT * HID + 1024].rearrange("p (a n) -> p a n", a=2)
        x1T_hi = ring_hi[:, :, :, :].rearrange("p a b c -> p (a b c)").rearrange("p (k n) -> p k n", k=KT2)
        x1T_lo = ring_lo[:, :, :, :].rearrange("p a b c -> p (a b c)").rearrange("p (k n) -> p k n", k=KT2)
        x1s = rpf[:, 0:1024].rearrange("p (a n) -> p a n", a=4)
        hbuf = eqkf[:, 0:1024].rearrange("p (a n) -> p a n", a=2)
        sg = rtf[:, 0:1024].rearrange("p (a n) -> p a n", a=2)
        lgT = oT[:, :]
        cmb = rqT[:, :].rearrange("p (a n) -> p a n", a=4)
        x2 = qkvf[:, 0:1024].rearrange("p (a n) -> p a n", a=4)
        xo = qkvf[:, 1024:2048].rearrange("p (a n) -> p a n", a=4)

        S = pb("S", [P128, 4, 512])
        PR = pb("PR", [P128, 1024])
        OA = pb("OA", [P128, 512])
        MS = pb("MS", [P128, 512])

        n_piece = 10
        s_raw = [sem(f"s_raw{i}") for i in range(n_piece)]
        s_sphi, s_splo = sem("s_sphi"), sem("s_splo")
        s_cst, s_wo, s_xin, s_zero, s_tab = (sem(n) for n in ("s_cst", "s_wo", "s_xin", "s_zero", "s_tab"))
        s_xr = [sem(f"s_xr{i}") for i in range(C)]
        s_proj, s_cp, s_mx, s_eq, s_na, s_ea, s_ln = (sem(n) for n in ("s_proj", "s_cp", "s_mx", "s_eq", "s_na", "s_ea", "s_ln"))
        s_re, s_gl, s_rt, s_rp = (sem(n) for n in ("s_re", "s_gl", "s_rt", "s_rp"))
        s_g, s_gc, s_eg, s_qd = (sem(n) for n in ("s_g", "s_gc", "s_eg", "s_qd"))
        s_trq, s_trd, s_trk, s_rqT, s_qdT, s_kT = (sem(n) for n in ("s_trq", "s_trd", "s_trk", "s_rqT", "s_qdT", "s_kT"))
        s_sc, s_nm, s_exp, s_rl, s_pn = (sem(n) for n in ("s_sc", "s_nm", "s_exp", "s_rl", "s_pn"))
        s_at, s_am, s_pt, s_wta, s_wtd = (sem(n) for n in ("s_at", "s_am", "s_pt", "s_wta", "s_wtd"))
        s_v, s_o, s_kv, s_kvr, s_U, s_oT, s_op, s_acc = (sem(n) for n in ("s_v", "s_o", "s_kv", "s_kvr", "s_U", "s_oT", "s_op", "s_acc"))
        s_wr = [sem(f"s_wr{i}") for i in range(4)]
        s_whi, s_wlo = sem("s_whi"), sem("s_wlo")
        s_bn, s_ve, s_rs, s_x1, s_x1a = (sem(n) for n in ("s_bn", "s_ve", "s_rs", "s_x1", "s_x1a"))
        s_t1, s_xhi, s_xlo, s_lgt, s_lgs, s_lg = (sem(n) for n in ("s_t1", "s_xhi", "s_xlo", "s_lgt", "s_lgs", "s_lg"))
        s_ro, s_lx, s_pe, s_cb, s_ctt, s_ct = (sem(n) for n in ("s_ro", "s_lx", "s_pe", "s_cb", "s_ctt", "s_ct"))
        s_gu, s_bc, s_sg, s_m, s_h, s_hhi, s_hlo, s_dn = (sem(n) for n in ("s_gu", "s_bc", "s_sg", "s_m", "s_h", "s_hhi", "s_hlo", "s_dn"))
        s_y, s_x2, s_b2, s_v2, s_r2, s_xo, s_out = (sem(n) for n in ("s_y", "s_x2", "s_b2", "s_v2", "s_r2", "s_xo", "s_out"))

        wv_hi = w_hi[:, :].rearrange("p (v n) -> p v n", v=KV)
        wv_lo = w_lo[:, :].rearrange("p (v n) -> p v n", v=KV)
        xv_hi = xT_hi[:, :].rearrange("p (k b n) -> p b k n", k=KT2, b=B)
        xv_lo = xT_lo[:, :].rearrange("p (k b n) -> p b k n", k=KT2, b=B)
        stA = prf[:, 0:KT2 * QKV]
        stB = wTf[:, 0:1024].rearrange("p (k n) -> p k n", k=KT2)
        stC = wTf[:, 1024:2048].rearrange("p (k n) -> p k n", k=KT2)
        xc = x_cols.rearrange("(k p) (b n) -> p b k n", p=P128, b=B)
        pieces = [
            (wqkv[:, 0], stA, wv_hi[:, 0], wv_lo[:, 0], None),
            (xc[:, 0], stB, xv_hi[:, 0], xv_lo[:, 0], None),
            (xc[:, 1], stC, xv_hi[:, 1], xv_lo[:, 1], None),
            (wqkv[:, 1], stA, wv_hi[:, 1], wv_lo[:, 1], 0),
            (xc[:, 2], stB, xv_hi[:, 2], xv_lo[:, 2], 1),
            (xc[:, 3], stC, xv_hi[:, 3], xv_lo[:, 3], 2),
            (wqkv[:, 2], stA, wv_hi[:, 2], wv_lo[:, 2], 3),
            (gate, wTf[:, 0:KT2 * E].rearrange("p (k e) -> p k e", k=KT2), gate_hi[:, :, 0:E], gate_lo[:, :, 0:E], 4),
            (wqkv[:, 3], stA, wv_hi[:, 3], wv_lo[:, 3], 6),
            (csel, prf[:, 0:FT * P128].rearrange("p (f c) -> p f c", f=FT), sel[:, :, :], None, 8),
        ]
        assert len(pieces) == n_piece

        def wq_cols(t, kv, k, a, b):
            v = t[:, :].rearrange("p (v k n) -> p v k n", v=KV, k=KT2)
            if isinstance(kv, int):
                return v[:, kv, k, a:b]
            return v[:, bass.ds(kv, 1), k, a:b].rearrange("p o n -> p (o n)")

        def kv_of(g, c):
            g2 = g + c // C
            return g2 % KV

        def tile_of(g, c):
            return ((g + c // C) // KV) * C + c % C

        def acc_tile(g, c):
            t = tile_of(g, c)
            if isinstance(t, int):
                return acc[:, t, :]
            return acc[:, bass.ds(t, 1), :].rearrange("p o n -> p (o n)")

        block = ctx.enter_context(nc.Block())

        @block.sync
        def _(sp):
            for i, (src, stage, hi, lo, prev) in enumerate(pieces):
                if prev is not None:
                    sp.wait_ge(s_sphi, prev + 1)
                    sp.wait_ge(s_splo, prev + 1)
                sp.dma_start(stage, src).then_inc(s_raw[i], 16)
                if i == 2:
                    sp.dma_start(cm[:, :], cmat).then_inc(s_cst, 16)
                    sp.dma_start(maskb[:, :, :], cmask).then_inc(s_cst, 16)
                    sp.dma_start(cos[:, :, :], rope_cos).then_inc(s_cst, 16)
                    sp.dma_start(sin[:, :, :], rope_sin).then_inc(s_cst, 16)
            sp.dma_start(acc[:, :, :], x_rows.rearrange("(t p) n -> p t n", p=P128)).then_inc(s_xin, 16)
            sp.dma_start(wo[:, :, :], wo_in).then_inc(s_wo, 16)

            xh = xT_hi[:, :].rearrange("p (k t) -> p k t", k=KT2)
            xl = xT_lo[:, :].rearrange("p (k t) -> p k t", k=KT2)

            def load_slot(g, c):
                later(sp, s_proj, C * g + c - C + 1)
                t = tile_of(g, c)
                cols = slice(t * P128, (t + 1) * P128) if isinstance(t, int) else bass.ds(t * P128, P128)
                sp.dma_start(ring_hi[:, c, :, :].bitcast(F32), xh[:, :, cols].bitcast(F32)).then_inc(s_xr[c], 16)
                sp.dma_start(ring_lo[:, c, :, :].bitcast(F32), xl[:, :, cols].bitcast(F32)).then_inc(s_xr[c], 16)

            sp.wait_ge(s_sphi, 2)
            sp.wait_ge(s_splo, 2)
            for c in range(C):
                load_slot(0, c)
            sp.wait_ge(s_sphi, 6)
            sp.wait_ge(s_splo, 6)
            with sp.Fori(1, NG) as g:
                for c in range(C):
                    load_slot(g, c)

            sp.wait_ge(s_o, NU)
            for f in range(FT):
                if f >= 4:
                    sp.wait_ge(s_whi, f - 3)
                    sp.wait_ge(s_wlo, f - 3)
                stage = (prf, wTf)[f % 4 // 2][:, 1024 * (f % 2):1024 * (f % 2) + 768]
                sp.dma_start(stage[:, 0:512], wgu[:, f]).then_inc(s_wr[f % 4], 16)
                sp.dma_start(stage[:, 512:768], wdn[:, f]).then_inc(s_wr[f % 4], 16)
            ov = out.rearrange("b (t p) n -> p (b t) n", p=P128)
            with sp.Fori(0, NGRP) as n:
                sp.wait_ge(s_xo, 4 * n + 4)
                sp.dma_start(ov[:, bass.ds(4 * n, 4), :], xo).then_inc(s_out, 16)
            sp.wait_ge(s_out, 16 * NGRP)

        @block.tensor
        def _(pe):
            def project(g, c):
                u = C * g + c
                cc = c % C
                kv = kv_of(g, c)
                pe.wait_ge(s_xr[cc], 32 * (g + c // C + 1))
                later(pe, s_cp, u)
                later(pe, s_rqT, u - 1)
                later(pe, s_qdT, u - 1)
                steps = [(k, x, w) for k in range(KT2) for x, w in ((ring_hi, w_hi), (ring_hi, w_lo), (ring_lo, w_hi))]
                for i, (k, x, w) in enumerate(steps):
                    for a, b in ((0, 512), (512, QKV)):
                        last = pe.matmul(PR[:, a:b], x[:, cc, k, :], wq_cols(w, kv, k, a, b),
                                         start=(i == 0), stop=(i == len(steps) - 1))
                last.then_inc(s_proj, 1)

            def gate_sums(g, c):
                u = C * g + c
                cc = c % C
                pe.wait_ge(s_gl, u + 1)
                later(pe, s_kT, 2 * u)
                if c - 2 < C - 1:
                    later(pe, s_kvr, 3 * g + c - 1)
                last = pe.matmul(MS[:, 0:128], gmat, gl[:, c % 2, :], start=True, stop=True)
                if cc > 0:
                    pe.matmul(MS[:, 128:129], gl[:, 1 - c % 2, :], late, start=True, stop=False)
                    last = pe.matmul(MS[:, 128:129], gl[:, c % 2, :], early, start=False, stop=True)
                last.then_inc(s_g, 1)

            def turn(g, c, has_next):
                u = C * g + c
                par = c % 2
                pe.wait_ge(s_rp, u + 1)
                if has_next:
                    pe.wait_ge(s_cp, u + 2)
                for h in range(GQ):
                    last = pe.transpose(PR[:, h * 128:(h + 1) * 128], rp[:, par, h * 128:(h + 1) * 128], ident)
                last.then_inc(s_trq, 1)
                pe.wait_ge(s_qd, 5 * (u + 1))
                for h in range(GQ):
                    last = pe.transpose(PR[:, 512 + h * 128:512 + (h + 1) * 128], qd[:, par, h * 128:(h + 1) * 128], ident)
                last.then_inc(s_trd, 1)
                pe.wait_ge(s_gc, u + 1)
                later(pe, s_acc, u - 1)
                pe.transpose(MS[:, 0:128], rp[:, par, 512:640], ident)
                pe.transpose(MS[:, 128:256], qd[:, par, 512:640], ident).then_inc(s_trk, 1)

            def score(g, c):
                u = C * g + c
                n = P128 * (c + 1)
                pe.wait_ge(s_rqT, u + 1)
                pe.wait_ge(s_kT, 2 * u + 2)
                later(pe, s_wta, 6 * g + tri(c - 1) if c else 6 * g)
                later(pe, s_wtd, u)
                for h in range(GQ):
                    pe.matmul(S[:, h, 0:n], rqT[:, h * 128:(h + 1) * 128], KT[:, 0:n], start=True, stop=False)
                    last = pe.matmul(S[:, h, n - 128:n], maskb[:, 0, :], maskb[:, 1, :], start=False, stop=True)
                    if h % 2:
                        last.then_inc(s_sc, 1)

            def gla_matrix(g, c):
                u = C * g + c
                later(pe, s_oT, u)
                pe.wait_ge(s_qdT, u + 1)
                pe.matmul(OA[:, :], kdT[:, :], qdT[:, c % 2, :], start=True, stop=True).then_inc(s_at, 1)

            def output(g, c):
                u = C * g + c
                kv = kv_of(g, c)
                pe.wait_ge(s_oT, u + 1)
                for h in range(GQ):
                    r = wo[:, kv * GQ + h, :] if isinstance(kv, int) else \
                        wo[:, bass.ds(kv * GQ + h, 1), :].rearrange("p o n -> p (o n)")
                    last = pe.matmul(MS[:, 0:HID], oT[:, h * 128:(h + 1) * 128], r, start=(h == 0), stop=(h == GQ - 1))
                last.then_inc(s_op, 1)

            def turn_weights(g, c):
                u = C * g + c
                pe.wait_ge(s_pn, 4 * (u + 1))
                for j in range(c + 1):
                    for h in range(GQ):
                        last = pe.transpose(S[:, j, h * 128:(h + 1) * 128], pr[:, h, j * 128:(j + 1) * 128], ident)
                    last.then_inc(s_pt, 1)

            def gather(g, c, has_next):
                u = C * g + c
                pe.wait_ge(s_am, u + 1)
                if c:
                    pe.wait_ge(s_U, 3 * g + c)
                    pe.matmul(OA[:, :], U[:, :], qdT[:, c % 2, :], start=True, stop=False)
                pe.wait_ge(s_v, u + 1)
                for j in range(c + 1):
                    if j < c:
                        pe.wait_ge(s_wta, 6 * g + tri(c - 1) + j + 1)
                    else:
                        pe.wait_ge(s_wtd, u + 1)
                    last = pe.matmul(OA[:, :], V[:, j, :], wT[:, j, :], start=(c == 0 and j == 0), stop=(j == c))
                last.then_inc(s_o, 1)
                if c < C - 1:
                    pe.wait_ge(s_kT, 2 * (u + 2))
                    pe.matmul(MS[:, 384:512], qd[:, c % 2, 512:640], V[:, c, :], start=True, stop=True).then_inc(s_kv, 1)

            def step(g, c, first=False, last=False):
                n1, n2 = not (last and c >= 3), not (last and c >= 2)
                score(g, c)
                gla_matrix(g, c)
                if n1:
                    gate_sums(g, c + 1)
                if n2:
                    project(g, c + 2)
                if n1:
                    pe.wait_ge(s_gc, C * g + c + 2)
                else:
                    pe.wait_ge(s_kvr, 3 * NG)
                if not (first and c == 0):
                    output(g - 1 if c == 0 else g, C - 1 if c == 0 else c - 1)
                turn_weights(g, c)
                if n1:
                    turn(g, c + 1, n2)
                gather(g, c, n1)

            pe.wait_ge(s_cst, 64)
            pe.wait_ge(s_sphi, 10)
            pe.wait_ge(s_splo, 9)
            project(0, 0)
            project(0, 1)
            gate_sums(0, 0)
            turn(0, 0, True)
            pe.wait_ge(s_wo, 16)
            for c in range(C):
                step(0, c, first=True)
            with pe.Fori(1, NG - 1) as g:
                for c in range(C):
                    step(g, c)
            for c in range(C):
                step(NG - 1, c, last=True)
            pe.wait_ge(s_acc, NU - 1)
            output(NG - 1, C - 1)

            def turn_x1(n, k):
                pe.wait_ge(s_x1, 4 * (n + 1))
                if k == 0:
                    later(pe, s_ct, n)
                    if isinstance(n, int) and n == 0:
                        pe.wait_ge(s_oT, NU)
                else:
                    pe.wait_ge(s_xlo, 2 * n + 1)
                for i in range(4):
                    last = pe.transpose(OA[:, i * 128:(i + 1) * 128], x1s[:, i, k * 128:(k + 1) * 128], ident)
                last.then_inc(s_t1, 1)

            def route(n):
                pe.wait_ge(s_xlo, 2 * n + 2)
                steps = [(k, w, x) for k in range(KT2) for w, x in ((gate_hi, x1T_hi), (gate_lo, x1T_hi), (gate_hi, x1T_lo))]
                for i, (k, w, x) in enumerate(steps):
                    last = pe.matmul(OA[:, :], w[:, k, :], x[:, k, :], start=(i == 0), stop=(i == len(steps) - 1))
                last.then_inc(s_lgt, 1)
                pe.wait_ge(s_lgs, n + 1)
                for i in range(4):
                    last = pe.transpose(OA[:, i * 128:(i + 1) * 128], lgT[:, i * 128:(i + 1) * 128], ident)
                last.then_inc(s_lg, 1)

            def turn_comb(n):
                pe.wait_ge(s_cb, n + 1)
                for i in range(4):
                    last = pe.transpose(OA[:, i * 128:(i + 1) * 128], cmb[:, i, :], ident)
                last.then_inc(s_ctt, 1)

            def gate_up(n, f):
                pe.wait_ge(s_wlo, f + 1)
                pe.wait_ge(s_xlo, 2 * n + 2)
                later(pe, s_m, FT * n + max(f - 1, 0))
                steps = [(k, w, x) for k in range(KT2) for w, x in ((gu_hi, x1T_hi), (gu_lo, x1T_hi), (gu_hi, x1T_lo))]
                for q in range(2):
                    for i, (k, w, x) in enumerate(steps):
                        last = pe.matmul(S[:, 2 * q + f % 2, :], w[:, f, k, q, :], x[:, k, :],
                                         start=(i == 0), stop=(i == len(steps) - 1))
                    last.then_inc(s_gu, 1)

            def spread_comb(n, f):
                pe.wait_ge(s_ct, n + 1)
                later(pe, s_h, FT * n + f)
                pe.matmul(MS[:, :], sel[:, f, :], combT, start=True, stop=True).then_inc(s_bc, 1)

            def down(n, f):
                pe.wait_ge(s_hhi, FT * n + f + 1)
                pe.wait_ge(s_hlo, FT * n + f + 1)
                if f == 0:
                    later(pe, s_x2, n)
                for i in range(4):
                    t = slice(i * 128, (i + 1) * 128)
                    for j, (hh, w) in enumerate(((hT_hi, dn_hi), (hT_hi, dn_lo), (hT_lo, dn_hi))):
                        last = pe.matmul(PR[:, i * 256:(i + 1) * 256], hh[:, f % 2, t], w[:, f, :],
                                         start=(f == 0 and j == 0 and i % 2 == 0), stop=(f == FT - 1 and j == 2),
                                         skip_group_check=True)
                last.then_inc(s_dn, 1)
                if f == FT - 1:
                    pass

            def group(n, more):
                for f in range(FT):
                    if f == FT - 1 and more:
                        turn_x1(n + 1, 0)
                    gate_up(n, f)
                    if f:
                        down(n, f - 1)
                    spread_comb(n, f)
                if more:
                    turn_x1(n + 1, 1)
                down(n, FT - 1)
                if more:
                    route(n + 1)
                    turn_comb(n + 1)

            turn_x1(0, 0)
            turn_x1(0, 1)
            route(0)
            pe.wait_ge(s_acc, NU)
            turn_comb(0)
            group(0, True)
            with pe.Fori(1, NGRP - 1) as n:
                group(n, True)
            group(NGRP - 1, False)

        @block.scalar
        def _(act):
            def o_out(g, c):
                u = C * g + c
                act.wait_ge(s_o, u + 1)
                later(act, s_op, u)
                nc.scalar.copy(oT[:, :], OA[:, :]).then_inc(s_oT, 1)

            def exps(g, c):
                u = C * g + c
                n = P128 * (c + 1)
                later(act, s_pt, 10 * g + tri(c))
                for h in range(GQ):
                    if h % 2 == 0:
                        act.wait_ge(s_nm, 2 * u + 1 + h // 2)
                    nc.scalar.activation(pr[:, h, 0:n], S[:, h, 0:n], ACT.Exp, bias=nm[:, h:h + 1], scale=1.0,
                                         accum_out=ls[:, h:h + 1]).then_inc(s_exp, 1)

            def exp_gates(g, c):
                u = C * g + c
                w = P128 + (1 if c % C else 0)
                act.wait_ge(s_gc, u + 1)
                par = c % 2
                nc.scalar.activation(eg[:, par, 0:w], gc[:, 0:w], ACT.Exp, scale=1.0 / GATE_NORM).then_inc(s_eg, 1)
                nc.scalar.activation(eg[:, par, 130:258], gc[:, 0:128], ACT.Exp, scale=-1.0 / GATE_NORM).then_inc(s_eg, 1)

            def copy_out(g, c):
                u = C * g + c
                act.wait_ge(s_proj, u + 1)
                later(act, s_v, u - 3)
                nc.scalar.copy(qkv[:, c % C, :], PR[:, 0:QKV]).then_inc(s_cp, 1)

            def features(g, c):
                u = C * g + c
                par = c % 2
                act.wait_ge(s_mx, u + 1)
                later(act, s_qd, 5 * (u - 1))
                later(act, s_re, u)
                for h in range(GQ + 1):
                    last = nc.scalar.activation(eqk[:, par, h * 128:(h + 1) * 128], qkv[:, c % C, h * 128:(h + 1) * 128],
                                                ACT.Exp, bias=nmx[:, h:h + 1], scale=1.0, accum_out=se[:, h:h + 1])
                last.then_inc(s_eq, 1)
                act.wait_ge(s_na, u + 1)
                nc.scalar.activation(eabs[:, :], nabs[:, :], ACT.Exp).then_inc(s_ea, 1)
                act.wait_ge(s_ea, u + 1)
                later(act, s_gl, u)
                nc.scalar.activation(lnp[:, :], eabs[:, :], ACT.Ln, bias=1.0).then_inc(s_ln, 1)

            def weights_out(g, c):
                u = C * g + c
                later(act, s_o, u)
                for j in range(c):
                    act.wait_ge(s_pt, 10 * g + tri(c) + j + 1)
                    nc.scalar.copy(wT[:, j, :], S[:, j, :]).then_inc(s_wta, 1)

            def turned_out(g, c):
                u = C * g + c
                act.wait_ge(s_trq, u + 1)
                later(act, s_sc, 2 * u)
                nc.scalar.copy(rqT[:, :], PR[:, 0:512]).then_inc(s_rqT, 1)
                act.wait_ge(s_trd, u + 1)
                later(act, s_o, u - 1)
                nc.scalar.copy(qdT[:, c % 2, :], PR[:, 512:1024]).then_inc(s_qdT, 1)

            def step(g, c, first=False, last=False):
                n1, n2 = not (last and c >= 3), not (last and c >= 2)
                if not (first and c == 0):
                    o_out(g - 1 if c == 0 else g, C - 1 if c == 0 else c - 1)
                exps(g, c)
                if n1:
                    exp_gates(g, c + 1)
                if n2:
                    copy_out(g, c + 2)
                    features(g, c + 2)
                weights_out(g, c)
                if n1:
                    turned_out(g, c + 1)

            act.preload_act_table_set("natural_log_exp_and_others")
            act.wait_ge(s_zero, 2)
            for i, (src, stage, hi, lo, prev) in enumerate(pieces):
                act.wait_ge(s_raw[i], 16)
                nc.scalar.copy(hi, stage).then_inc(s_sphi, 1)
            copy_out(0, 0)
            features(0, 0)
            copy_out(0, 1)
            features(0, 1)
            exp_gates(0, 0)
            turned_out(0, 0)
            act.wait_ge(s_splo, n_piece - 1)
            for c in range(C):
                step(0, c, first=True)
            with act.Fori(1, NG - 1) as g:
                for c in range(C):
                    step(g, c)
            for c in range(C):
                step(NG - 1, c, last=True)
            o_out(NG - 1, C - 1)

            def split_hi(f):
                act.wait_ge(s_wr[f % 4], 32 * (f // 4 + 1))
                stage = (prf, wTf)[f % 4 // 2][:, 1024 * (f % 2):1024 * (f % 2) + 768]
                nc.scalar.copy(gu_hi[:, f].rearrange("p k w c -> p (k w c)"), stage[:, 0:512])
                nc.scalar.copy(dn_hi[:, f, :], stage[:, 512:768]).then_inc(s_whi, 1)

            def x1_hi(n, k):
                act.wait_ge(s_t1, 2 * n + k + 1)
                if k == 0:
                    later(act, s_gu, 2 * FT * n)
                nc.scalar.copy(x1T_hi[:, k, :], OA[:, :]).then_inc(s_xhi, 1)

            def route_out(n):
                act.wait_ge(s_lgt, n + 1)
                if isinstance(n, int) and n == 0:
                    act.wait_ge(s_op, NU)
                nc.scalar.copy(lgT, OA[:, :]).then_inc(s_lgs, 1)
                act.wait_ge(s_lx, n + 1)
                nc.scalar.activation(pe_[:, :, :], lx[:, :, :], ACT.Exp).then_inc(s_pe, 1)

            def comb_out(n):
                act.wait_ge(s_ctt, n + 1)
                later(act, s_bc, FT * n)
                nc.scalar.copy(combT, OA[:, :]).then_inc(s_ct, 1)

            def silu(n, f):
                act.wait_ge(s_gu, 2 * (FT * n + f) + 2)
                later(act, s_m, FT * n + max(f - 1, 0))
                nc.scalar.activation(sg[:, f % 2, :], S[:, f % 2, :], ACT.Silu).then_inc(s_sg, 1)

            def h_hi(n, f):
                act.wait_ge(s_h, FT * n + f + 1)
                later(act, s_dn, FT * n + max(f - 1, 0))
                nc.scalar.copy(hT_hi[:, f % 2, :], hbuf[:, f % 2, :]).then_inc(s_hhi, 1)

            def group(n, more):
                for f in range(FT):
                    silu(n, f)
                    h_hi(n, f)
                if more:
                    x1_hi(n + 1, 0)
                    x1_hi(n + 1, 1)
                    route_out(n + 1)
                    comb_out(n + 1)

            for f in range(3):
                split_hi(f)
            x1_hi(0, 0)
            x1_hi(0, 1)
            for f in range(3, 7):
                split_hi(f)
            route_out(0)
            for f in range(7, FT):
                split_hi(f)
            comb_out(0)
            group(0, True)
            with act.Fori(1, NGRP - 1) as n:
                group(n, True)
            group(NGRP - 1, False)

        @block.vector
        def _(dve):
            def exp_view(t):
                return t.rearrange("p (h d) -> p h d", d=128)

            def move_v(g, c):
                u = C * g + c
                later(dve, s_o, u)
                nc.vector.tensor_copy(V[:, c, :], qkv[:, c, 640:768]).then_inc(s_v, 1)

            def score_max(g, c, pair):
                u = C * g + c
                n = P128 * (c + 1)
                dve.wait_ge(s_sc, 2 * u + 1 + pair)
                later(dve, s_exp, 4 * u)
                nc.vector.tensor_reduce(nm[:, 2 * pair:2 * pair + 2], S[:, 2 * pair:2 * pair + 2, 0:n], AX_X, ALU.max,
                                        negate=True).then_inc(s_nm, 1)

            def mask_gla(g, c):
                u = C * g + c
                dve.wait_ge(s_at, u + 1)
                nc.vector.tensor_tensor(exp_view(am[:, :]), exp_view(OA[:, :]),
                                        keep.rearrange("p (o t) -> p o t", o=1).to_broadcast([P128, GQ, P128]),
                                        ALU.mult).then_inc(s_am, 1)

            def update_state(g, c):
                u = C * g + c
                dve.wait_ge(s_kv, 3 * g + c)
                dve.wait_ge(s_eg, 2 * (u + 1))
                r = eg[:, c % 2, 128:129]
                if c == 1:
                    nc.vector.tensor_copy(Ut[:, :], MS[:, 384:512]).then_inc(s_kvr, 1)
                else:
                    nc.vector.tensor_tensor(Ut[:, :], MS[:, 384:512], U[:, :], ALU.add).then_inc(s_kvr, 1)
                dve.wait_ge(s_kvr, 3 * g + c)
                later(dve, s_o, u)
                nc.vector.tensor_scalar(U[:, :], Ut[:, :], r, None, ALU.mult).then_inc(s_U, 1)

            def normalise(g, c, pair):
                u = C * g + c
                n = P128 * (c + 1)
                dve.wait_ge(s_exp, 4 * u + 2 * pair + 2)
                nc.vector.reciprocal(rl[:, 2 * pair:2 * pair + 2], ls[:, 2 * pair:2 * pair + 2]).then_inc(s_rl, 1)
                dve.wait_ge(s_rl, 2 * u + pair + 1)
                for h in (2 * pair, 2 * pair + 1):
                    nc.vector.tensor_scalar(pr[:, h, 0:n], pr[:, h, 0:n], rl[:, h:h + 1], None, ALU.mult).then_inc(s_pn, 1)

            def clamp_gates(g, c):
                u = C * g + c
                w = P128 + (1 if c % C else 0)
                dve.wait_ge(s_g, u + 1)
                later(dve, s_eg, 2 * u)
                nc.vector.tensor_scalar(gc[:, 0:w], MS[:, 0:w], -GCLAMP, GCLAMP, ALU.max, ALU.min).then_inc(s_gc, 1)

            def decay(g, c):
                u = C * g + c
                par = c % 2
                dve.wait_ge(s_eg, 2 * (u + 1))
                dve.wait_ge(s_re, u + 1)
                later(dve, s_trk, u - 1)
                if (c - 2) % C < C - 1:
                    later(dve, s_kv, kv_count(g, c - 2))
                for h in range(GQ + 1):
                    e = eg[:, par, 0:128] if h < GQ else eg[:, par, 130:258]
                    nc.vector.scalar_tensor_tensor(out=qd[:, par, h * 128:(h + 1) * 128], in0=eqk[:, par, h * 128:(h + 1) * 128],
                                                   scalar=rse[:, par, h:h + 1], in1=e, op0=ALU.mult,
                                                   op1=ALU.mult).then_inc(s_qd, 1)

            def kv_count(g, c):
                return 3 * g + c + 1 if c >= 0 else 3 * g + min(c + 1, 0)

            def add_output(g, c):
                u = C * g + c
                dve.wait_ge(s_op, u + 1)
                a = acc_tile(g, c)
                nc.vector.scalar_tensor_tensor(out=a, in0=MS[:, 0:HID], scalar=0.5, in1=a, op0=ALU.mult,
                                               op1=ALU.add).then_inc(s_acc, 1)

            def prepare(g, c):
                u = C * g + c
                x = qkv[:, c % C, 0:QK]
                dve.wait_ge(s_cp, u + 1)
                later(dve, s_eq, u)
                nc.vector.tensor_reduce(nmx[:, :], exp_view(x), AX_X, ALU.max, negate=True).then_inc(s_mx, 1)
                later(dve, s_ea, u)
                k = qkv[:, c % C, 512:640]
                nc.vector.scalar_tensor_tensor(out=nabs[:, :], in0=k, scalar=-1.0, in1=k, op0=ALU.mult,
                                               op1=ALU.min).then_inc(s_na, 1)
                later(dve, s_rp, u)
                x4 = x.rearrange("p (h w d) -> p h w d", w=2, d=64)
                for i, (t, src) in enumerate(((cos, x4), (sin, x4[:, :, ::-1, :]))):
                    tab = t[:, c % C, :].rearrange("p (o w d) -> p o w d", o=1, w=2).to_broadcast([P128, GQ + 1, 2, 64])
                    nc.vector.tensor_tensor(rt[:, i, :].rearrange("p (h w d) -> p h w d", w=2, d=64), src, tab,
                                            ALU.mult).then_inc(s_rt, 1)

            def add_gla(g, c):
                u = C * g + c
                dve.wait_ge(s_pt, 10 * g + tri(c) + c + 1)
                dve.wait_ge(s_am, u + 1)
                later(dve, s_o, u)
                nc.vector.tensor_tensor(wT[:, c, :], S[:, c, :], am[:, :], ALU.add).then_inc(s_wtd, 1)

            def k_out(g, c):
                u = C * g + c
                dve.wait_ge(s_trk, u + 1)
                later(dve, s_sc, 2 * u)
                later(dve, s_at, u)
                nc.vector.tensor_copy(KT[:, (c % C) * 128:(c % C + 1) * 128], MS[:, 0:128]).then_inc(s_kT, 1)
                nc.vector.tensor_copy(kdT[:, :], MS[:, 128:256]).then_inc(s_kT, 1)

            def log_gates(g, c):
                u = C * g + c
                par = c % 2
                dve.wait_ge(s_eq, u + 1)
                later(dve, s_qd, 5 * (u - 1))
                nc.vector.reciprocal(rse[:, par, :], se[:, :]).then_inc(s_re, 1)
                dve.wait_ge(s_ln, u + 1)
                later(dve, s_g, u)
                nc.vector.scalar_tensor_tensor(out=gl[:, par, :], in0=qkv[:, c % C, 512:640], scalar=0.0, in1=lnp[:, :],
                                               op0=ALU.min, op1=ALU.subtract).then_inc(s_gl, 1)

            def step(g, c, first=False, last=False):
                n1, n2 = not (last and c >= 3), not (last and c >= 2)
                if c:
                    update_state(g, c)
                score_max(g, c, 0)
                score_max(g, c, 1)
                mask_gla(g, c)
                normalise(g, c, 0)
                move_v(g, c)
                if n1:
                    clamp_gates(g, c + 1)
                normalise(g, c, 1)
                if n1:
                    decay(g, c + 1)
                if n2:
                    prepare(g, c + 2)
                if not (first and c == 0):
                    add_output(g - 1 if c == 0 else g, C - 1 if c == 0 else c - 1)
                add_gla(g, c)
                if n1:
                    k_out(g, c + 1)
                if n2:
                    log_gates(g, c + 2)

            nc.vector.memset(gate_hi[:, :, :].bitcast(F32), 0.0).then_inc(s_zero, 1)
            nc.vector.memset(gate_lo[:, :, :].bitcast(F32), 0.0).then_inc(s_zero, 1)
            dve.wait_ge(s_zero, 2)
            for i, (src, stage, hi, lo, prev) in enumerate(pieces):
                if lo is None:
                    continue
                dve.wait_ge(s_sphi, i + 1)
                nc.vector.tensor_tensor(lo, stage, hi.bitcast(F32), ALU.subtract).then_inc(s_splo, 1)
            dve.wait_ge(s_cst, 64)
            prepare(0, 0)
            log_gates(0, 0)
            prepare(0, 1)
            log_gates(0, 1)
            clamp_gates(0, 0)
            decay(0, 0)
            k_out(0, 0)
            dve.wait_ge(s_xin, 16)
            for c in range(C):
                step(0, c, first=True)
            with dve.Fori(1, NG - 1) as g:
                for c in range(C):
                    step(g, c)
            for c in range(C):
                step(NG - 1, c, last=True)
            add_output(NG - 1, C - 1)

            def tile_at(n, i):
                if isinstance(n, int):
                    return acc[:, 4 * n + i, :]
                return acc[:, bass.ds(4 * n + i, 1), :].rearrange("p o n -> p (o n)")

            def split_lo(f):
                dve.wait_ge(s_whi, f + 1)
                stage = (prf, wTf)[f % 4 // 2][:, 1024 * (f % 2):1024 * (f % 2) + 768]
                nc.vector.tensor_tensor(gu_lo[:, f].rearrange("p k w c -> p (k w c)"), stage[:, 0:512],
                                        gu_hi[:, f].rearrange("p k w c -> p (k w c)").bitcast(F32), ALU.subtract)
                nc.vector.tensor_tensor(dn_lo[:, f, :], stage[:, 512:768], dn_hi[:, f, :].bitcast(F32),
                                        ALU.subtract).then_inc(s_wlo, 1)

            def held(sem_, value):
                dve.wait_ge(sem_, value)
                nc.vector.memset(pad[:, :], 0.0)

            def norm1(n):
                for i in range(4):
                    nc.vector.bn_stats(st[:, i, :], tile_at(n, i)).then_inc(s_bn, 1)
                held(s_bn, 8 * n + 4)
                for i in range(4):
                    nc.vector.bn_aggr(mv[:, i, :], st[:, i, :]).then_inc(s_bn, 1)
                dve.wait_ge(s_bn, 8 * n + 8)
                nc.vector.tensor_scalar(ve[:, :], mv[:, :, 1], EPS, None, ALU.add).then_inc(s_ve, 1)
                dve.wait_ge(s_rs, n + 1)
                later(dve, s_t1, 2 * n)
                for i in range(4):
                    nc.vector.tensor_scalar(x1s[:, i, :], tile_at(n, i), mv[:, i, 0:1], rstd[:, i:i + 1],
                                            ALU.subtract, ALU.mult).then_inc(s_x1, 1)
                for i in range(4):
                    nc.vector.tensor_scalar(tile_at(n, i), tile_at(n, i), mv[:, i, 0:1], rstd[:, i:i + 1],
                                            ALU.subtract, ALU.mult).then_inc(s_x1a, 1)

            def x1_lo(n, k):
                dve.wait_ge(s_xhi, 2 * n + k + 1)
                nc.vector.tensor_tensor(x1T_lo[:, k, :], OA[:, :], x1T_hi[:, k, :].bitcast(F32),
                                        ALU.subtract).then_inc(s_xlo, 1)

            ro = [0]

            def route_dve(n):
                base = 13 * n
                k = [0]

                def link(ins):
                    k[0] += 1
                    ins.then_inc(s_ro, 1)
                    dve.wait_ge(s_ro, base + k[0])

                dve.wait_ge(s_lg, n + 1)
                link(nc.vector.tensor_copy(lg[:, :, :], OA[:, :].rearrange("p (a n) -> p a n", a=4)[:, :, 0:E]))
                link(nc.vector.tensor_reduce(small[:, 0:4], lg[:, :, :], AX_X, ALU.max))
                nc.vector.tensor_tensor(lx[:, :, :], lg[:, :, :], small[:, 0:4].rearrange("p (a o) -> p a o", o=1)
                                        .to_broadcast([P128, 4, E]), ALU.subtract).then_inc(s_lx, 1)
                me = lg[:, :, :].rearrange("p a (e o) -> p a e o", o=1).to_broadcast([P128, 4, E, E])
                you = lg[:, :, :].rearrange("p a (o e) -> p a o e", o=1).to_broadcast([P128, 4, E, E])
                r1 = rk1[:, :].rearrange("p (a e f) -> p a e f", a=4, e=E)
                r2 = rk2[:, :].rearrange("p (a e f) -> p a e f", a=4, e=E)
                link(nc.vector.tensor_tensor(r1, you, me, ALU.is_gt))
                link(nc.vector.tensor_tensor(r2, you, me, ALU.is_equal))
                link(nc.vector.tensor_tensor(r2, r2, tri8[:, :, :].rearrange("p (o e) f -> p o e f", o=1)
                                             .to_broadcast([P128, 4, E, E]), ALU.mult))
                link(nc.vector.tensor_tensor(rk1[:, :], rk1[:, :], rk2[:, :], ALU.add))
                link(nc.vector.tensor_reduce(rank[:, :, :], r1, AX_X, ALU.add))
                link(nc.vector.tensor_scalar(topm[:, :, :], rank[:, :, :], 2.0, None, ALU.is_lt))
                dve.wait_ge(s_pe, n + 1)
                link(nc.vector.tensor_reduce(small[:, 4:8], pe_[:, :, :], AX_X, ALU.add))
                link(nc.vector.reciprocal(small[:, 8:12], small[:, 4:8]))
                link(nc.vector.tensor_tensor(comb[:, :, :], pe_[:, :, :], topm[:, :, :], ALU.mult))
                link(nc.vector.tensor_tensor(comb[:, :, :], comb[:, :, :], small[:, 8:12]
                                             .rearrange("p (a o) -> p a o", o=1).to_broadcast([P128, 4, E]), ALU.mult))
                link(nc.vector.tensor_copy(cmb[:, :, 0:E].bitcast(F32R), comb[:, :, :]))
                nc.vector.tensor_tensor(cmb[:, :, E:2 * E], comb[:, :, :], cmb[:, :, 0:E], ALU.subtract).then_inc(s_cb, 1)
                assert k[0] == 13

            def multiply(n, f):
                dve.wait_ge(s_sg, FT * n + f + 1)
                nc.vector.tensor_tensor(am[:, :], sg[:, f % 2, :], S[:, 2 + f % 2, :], ALU.mult).then_inc(s_m, 1)
                dve.wait_ge(s_m, FT * n + f + 1)
                dve.wait_ge(s_bc, FT * n + f + 1)
                later(dve, s_hhi, FT * n + max(f - 1, 0))
                nc.vector.tensor_tensor(hbuf[:, f % 2, :], am[:, :], MS[:, :], ALU.mult).then_inc(s_h, 1)

            def h_lo(n, f):
                dve.wait_ge(s_hhi, FT * n + f + 1)
                later(dve, s_dn, FT * n + max(f - 1, 0))
                nc.vector.tensor_tensor(hT_lo[:, f % 2, :], hbuf[:, f % 2, :], hT_hi[:, f % 2, :].bitcast(F32),
                                        ALU.subtract).then_inc(s_hlo, 1)

            def norm2(n):
                dve.wait_ge(s_dn, FT * (n + 1))
                later(dve, s_x1a, 4 * n + 4)
                a = acc[:, 4 * n:4 * n + 4, :] if isinstance(n, int) else acc[:, bass.ds(4 * n, 4), :]
                nc.vector.tensor_tensor(x2.rearrange("p a n -> p (a n)"), PR[:, :], a.rearrange("p a n -> p (a n)"),
                                        ALU.add).then_inc(s_x2, 1)
                dve.wait_ge(s_x2, n + 1)
                for i in range(4):
                    nc.vector.bn_stats(st2[:, i, :], x2[:, i, :]).then_inc(s_b2, 1)
                held(s_b2, 8 * n + 4)
                for i in range(4):
                    nc.vector.bn_aggr(mv2[:, i, :], st2[:, i, :]).then_inc(s_b2, 1)
                dve.wait_ge(s_b2, 8 * n + 8)
                nc.vector.tensor_scalar(ve2[:, :], mv2[:, :, 1], EPS, None, ALU.add).then_inc(s_v2, 1)
                dve.wait_ge(s_r2, n + 1)
                later(dve, s_out, 16 * n)
                for i in range(4):
                    nc.vector.tensor_scalar(xo[:, i, :], x2[:, i, :], mv2[:, i, 0:1], rstd2[:, i:i + 1],
                                            ALU.subtract, ALU.mult).then_inc(s_xo, 1)

            def group(n, more):
                for f in range(FT):
                    multiply(n, f)
                    h_lo(n, f)
                    if f == 5 and more:
                        norm1(n + 1)
                if more:
                    x1_lo(n + 1, 0)
                    x1_lo(n + 1, 1)
                    route_dve(n + 1)
                norm2(n)

            dve.wait_ge(s_acc, NU)
            norm1(0)
            for f in range(3):
                split_lo(f)
            x1_lo(0, 0)
            x1_lo(0, 1)
            for f in range(3, 7):
                split_lo(f)
            nc.vector.memset(rqT[:, :], 0.0).then_inc(s_zero, 1)
            dve.wait_ge(s_zero, 3)
            dve.wait_ge(s_tab, 2)
            route_dve(0)
            for f in range(7, FT):
                split_lo(f)
            group(0, True)
            with dve.Fori(1, NGRP - 1) as n:
                group(n, True)
            group(NGRP - 1, False)

        @block.gpsimd
        def _(pool):
            def rotate(g, c):
                u = C * g + c
                par = c % 2
                pool.wait_ge(s_rt, 2 * (u + 1))
                later(pool, s_trk, u - 1)
                nc.gpsimd.tensor_tensor(rp[:, par, :], rt[:, 0, :], rt[:, 1, :], ALU.add).then_inc(s_rp, 1)

            def step(g, c, last=False):
                if not (last and c >= 2):
                    rotate(g, c + 2)

            nc.gpsimd.memset(neghalf[:, :], -0.5).then_inc(s_tab, 1)
            for e in range(E):
                if e:
                    nc.gpsimd.memset(tri8[:, e, 0:e], 1.0)
                last = nc.gpsimd.memset(tri8[:, e, e:E], 0.0)
            last.then_inc(s_tab, 1)
            rotate(0, 0)
            rotate(0, 1)
            for c in range(C):
                step(0, c)
            with pool.Fori(1, NG - 1) as g:
                for c in range(C):
                    step(g, c)
            for c in range(C):
                step(NG - 1, c, last=True)

            def rs1(n):
                pool.wait_ge(s_ve, n + 1)
                nc.gpsimd.tensor_tensor(rstd[:, :], ve[:, :], neghalf[:, :], ALU.pow).then_inc(s_rs, 1)

            def rs2(n):
                pool.wait_ge(s_v2, n + 1)
                nc.gpsimd.tensor_tensor(rstd2[:, :], ve2[:, :], neghalf[:, :], ALU.pow).then_inc(s_r2, 1)

            pool.wait_ge(s_tab, 2)
            rs1(0)
            with pool.Fori(0, NGRP - 1) as n:
                rs1(n + 1)
                rs2(n)
            rs2(NGRP - 1)


def kernel(L0_attn_hidden_states, L0_attn_Wq, L0_attn_Wk, L0_attn_Wv, L0_attn_Wo, L0_ffn_gate_w, L0_ffn_w_gate,
           L0_ffn_w_up, L0_ffn_w_down):
    import numpy as np
    import concourse.bacc as bacc
    from concourse.bass_utils import run_bass_kernel_spmd

    x = np.ascontiguousarray(L0_attn_hidden_states).reshape(B * N, HID)

    def by_kv(w, heads):
        return w.reshape(KT2, P128, KV, heads * D).transpose(1, 2, 0, 3)

    wqkv = np.concatenate([by_kv(np.asarray(L0_attn_Wq), GQ), by_kv(np.asarray(L0_attn_Wk), 1),
                           by_kv(np.asarray(L0_attn_Wv), 1)], axis=3)
    wo = np.asarray(L0_attn_Wo).reshape(H, D, HID).transpose(1, 0, 2)

    def features(w):
        return np.asarray(w).transpose(1, 0, 2).reshape(KT2, P128, FT, P128).transpose(1, 2, 0, 3)

    wgu = np.stack([features(L0_ffn_w_gate), features(L0_ffn_w_up)], axis=3)
    wdn = np.asarray(L0_ffn_w_down).reshape(FT, P128, HID).transpose(1, 0, 2)
    gate = np.asarray(L0_ffn_gate_w).T.reshape(KT2, P128, E).transpose(1, 0, 2)

    f32 = np.float32
    inv_freq = (f32(1.0) / f32(10000.0) ** (np.arange(0, D, 2, dtype=f32) / f32(D))).astype(f32)
    ang = np.arange(N, dtype=f32)[:, None] * inv_freq[None, :]
    root = np.sqrt(np.sqrt(1.0 / D))
    cos = (np.cos(ang.astype(np.float64)) * root).reshape(C, P128, D // 2).transpose(1, 0, 2)
    sin = (np.sin(ang.astype(np.float64)) * root).reshape(C, P128, D // 2).transpose(1, 0, 2)
    cos2 = np.concatenate([cos, cos], axis=2).astype(f32)
    sin2 = np.concatenate([-sin, sin], axis=2).astype(f32)
    s = np.arange(P128)[:, None]
    t = np.arange(P128)[None, :]
    cmat = np.concatenate([s == t, s <= t, (s <= t).astype(f32) - (s < 64), s < 64, s >= 64], axis=1).astype(f32)
    bf16 = mybir.dt.np(BF16)
    cmask = np.stack([(s == t).astype(f32), np.where(t > s, f32(NEG), f32(0.0))], axis=1).astype(bf16)
    expert = (np.arange(E * F) // F).reshape(FT, P128)
    csel = np.zeros((P128, FT, P128), f32)
    for e in range(E):
        csel[e] = expert == e
        csel[E + e] = expert == e

    named = {"x_rows": x, "x_cols": x.T, "wqkv": wqkv, "wo_in": wo, "wgu": wgu.reshape(P128, FT, KT2 * 2 * P128),
             "wdn": wdn, "gate": gate, "rope_cos": cos2, "rope_sin": sin2, "cmat": cmat, "cmask": cmask, "csel": csel}
    named["wqkv"] = wqkv.reshape(P128, KV, KT2 * QKV)
    nc = bacc.Bacc("TRN2", target_bir_lowering=False, num_devices=1)
    arrays, aps = {}, {}
    for name, a in named.items():
        a = np.ascontiguousarray(a)
        arrays["in_" + name] = a
        aps[name] = nc.dram_tensor("in_" + name, a.shape, mybir.dt.from_np(a.dtype), kind="ExternalInput").ap()
    out = nc.dram_tensor("out_0", (B, N, HID), F32, kind="ExternalOutput").ap()
    layer_kernel(nc, out=out, **aps)
    r = run_bass_kernel_spmd(nc, [arrays], core_ids=[0])
    return r.results[0]["out_0"]
```

```python
from contextlib import ExitStack

import concourse.bass as bass
from concourse import mybir

F32 = mybir.dt.float32
F32R = mybir.dt.float32r
BF16 = mybir.dt.bfloat16
ALU = mybir.AluOpType
ACT = mybir.ActivationFunctionType
AX_X = mybir.AxisListType.X

P128 = 128
B, N, HID = 4, 512, 256
H, KV, D = 16, 4, 128
GQ = H // KV
C = N // P128
NG = B * KV
NU = NG * C
KT2 = HID // P128
QKV = GQ * D + 2 * D
QK = GQ * D + D
GATE_NORM = 16.0
GCLAMP = 80.0 * GATE_NORM
EPS = 1e-5
E, F = 8, 176
FT = E * F // P128
TILES = B * N // P128
NGRP = B * N // 512
NEG = -1.0e30
WJOB = KT2 * 2 * P128 + HID
assert WJOB == QKV


def later(eng, sem, value):
    if isinstance(value, int) and value <= 0:
        return
    eng.wait_ge(sem, value)


def tri(c):
    return c * (c + 1) // 2


def layer_kernel(nc, x_rows, x_cols, wqkv, wo_in, wffn, gate, rope_cos, rope_sin, cmat, cmask, csel, out):
    with ExitStack() as ctx:
        def sb(name, shape, dt):
            return ctx.enter_context(nc.sbuf_tensor(name, shape, dt))

        def pb(name, shape):
            return ctx.enter_context(nc.psum_tensor(name, shape, F32))

        def sem(name):
            return ctx.enter_context(nc.semaphore(name))

        w_hi = sb("w_hi", [P128, KV * KT2 * QKV], F32R)
        w_lo = sb("w_lo", [P128, KV * KT2 * QKV], F32R)
        wo_hi = sb("wo_hi", [P128, H * HID], F32R)
        wo_lo = sb("wo_lo", [P128, H * HID], F32R)
        stage = sb("stage", [P128, 2, WJOB], F32)
        acc = sb("acc", [P128, TILES, HID], F32)
        cos = sb("cos", [P128, C, D], F32)
        sin = sb("sin", [P128, C, D], F32)
        gate_hi = sb("gate_hi", [P128, KT2, P128], F32R)
        gate_lo = sb("gate_lo", [P128, KT2, P128], F32R)
        cm = sb("cm", [P128, 3 * P128 + 2], F32)
        ident = cm[:, 0:128]
        keep = cm[:, 128:256]
        gmat = cm[:, 256:384]
        halves = cm[:, 384:386]
        maskb = sb("maskb", [P128, 2, P128], BF16)
        tri8 = sb("tri8", [P128, E, E], F32)
        neghalf = sb("neghalf", [P128, C], F32)

        ring_hi = sb("ring_hi", [P128, 2048], F32R)
        ring_lo = sb("ring_lo", [P128, 2048], F32R)
        xraw = sb("xraw", [P128, 2, KT2, P128], F32)
        qkv = sb("qkv", [P128, C, QKV], F32)
        eqk = sb("eqk", [P128, 2, QK], F32)
        rt = sb("rt", [P128, QK], F32)
        rp = sb("rp", [P128, 2, QK], F32)
        qd = sb("qd", [P128, 2, QK], F32)
        rqT = sb("rqT", [P128, GQ * P128], F32)
        k0T = sb("k0T", [P128, P128], F32)
        rq_hi = sb("rq_hi", [P128, GQ * P128], F32R)
        rq_lo = sb("rq_lo", [P128, GQ * P128], F32R)
        KT_hi = sb("KT_hi", [P128, C * P128], F32R)
        KT_lo = sb("KT_lo", [P128, C * P128], F32R)
        qdT = sb("qdT", [P128, 2, GQ * P128], F32)
        kdT = sb("kdT", [P128, P128], F32)
        pr = sb("pr", [P128, GQ, N], F32)
        wT = sb("wT", [P128, C, GQ * P128], F32)
        am = sb("am", [P128, GQ * P128], F32)
        oT_hi = sb("oT_hi", [P128, GQ * P128], F32R)
        oT_lo = sb("oT_lo", [P128, GQ * P128], F32R)
        V = sb("V", [P128, C, D], F32)
        U = sb("U", [P128, D], F32)
        Ut = sb("Ut", [P128, D], F32)
        eg = sb("eg", [P128, 2, 2 * P128 + 2], F32)
        gc = sb("gc", [P128, P128 + 2], F32)
        gl = sb("gl", [P128, D], F32)
        nabs = sb("nabs", [P128, D], F32)
        eabs = sb("eabs", [P128, D], F32)
        lnp = sb("lnp", [P128, D], F32)
        nmx = sb("nmx", [P128, GQ + 1], F32)
        se = sb("se", [P128, GQ + 1], F32)
        rse = sb("rse", [P128, 2, GQ + 1], F32)
        nm = sb("nm", [P128, GQ], F32)
        ls = sb("ls", [P128, GQ], F32)
        rl = sb("rl", [P128, GQ], F32)
        st = [None] + [sb(f"st{i}", [P128, 4, 6], F32) for i in (1, 2)]
        mv = [None] + [sb(f"mv{i}", [P128, 4, 2], F32) for i in (1, 2)]
        ve = [None] + [sb(f"ve{i}", [P128, 4], F32) for i in (1, 2)]
        rstd = [None] + [sb(f"rstd{i}", [P128, 4], F32) for i in (1, 2)]
        lg = sb("lg", [P128, 4, E], F32)
        lx = sb("lx", [P128, 4, E], F32)
        pe_ = sb("pe_", [P128, 4, E], F32)
        rank = sb("rank", [P128, 4, E], F32)
        topm = sb("topm", [P128, 4, E], F32)
        comb = sb("comb", [P128, 4, E], F32)
        small = sb("small", [P128, 12], F32)
        rk1 = sb("rk1", [P128, 4 * E * E], F32)
        rk2 = sb("rk2", [P128, 4 * E * E], F32)

        prf = pr[:, :, :].rearrange("p a b -> p (a b)")
        wTf = wT[:, :, :].rearrange("p a b -> p (a b)")
        qkvf = qkv[:, :, :].rearrange("p a b -> p (a b)")
        eqkf = eqk[:, :, :].rearrange("p a b -> p (a b)")
        rpf = rp[:, :, :].rearrange("p a b -> p (a b)")

        gu_hi = w_hi[:, 0:FT * KT2 * 2 * P128].rearrange("p (f k w c) -> p f k w c", f=FT, k=KT2, w=2)
        gu_lo = w_lo[:, 0:FT * KT2 * 2 * P128].rearrange("p (f k w c) -> p f k w c", f=FT, k=KT2, w=2)
        combT = w_hi[:, FT * KT2 * 2 * P128:FT * KT2 * 2 * P128 + 512]
        dn_hi = wo_hi[:, 0:FT * HID].rearrange("p (f n) -> p f n", f=FT)
        dn_lo = wo_lo[:, 0:FT * HID].rearrange("p (f n) -> p f n", f=FT)
        hT_hi = wo_hi[:, 3072:4096].rearrange("p (a n) -> p a n", a=2)
        hT_lo = wo_lo[:, 3072:4096].rearrange("p (a n) -> p a n", a=2)
        x1T_hi = ring_hi[:, :].rearrange("p (a k n) -> p a k n", a=2, k=KT2)
        x1T_lo = ring_lo[:, :].rearrange("p (a k n) -> p a k n", a=2, k=KT2)
        x1s = qkvf[:, 0:1024].rearrange("p (a n) -> p a n", a=4)
        hbuf = eqkf[:, 0:1024].rearrange("p (a n) -> p a n", a=2)
        sg = wTf[:, 0:1024].rearrange("p (a n) -> p a n", a=2)
        lgT = qdT[:, 0, :]
        cmb = rqT[:, :].rearrange("p (a n) -> p a n", a=4)
        x2 = rpf[:, 0:1024].rearrange("p (a n) -> p a n", a=4)
        xo = prf[:, 0:1024].rearrange("p (a n) -> p a n", a=4)

        xs_hi = ring_hi[:, 0:1024].rearrange("p (c k n) -> p c k n", c=C, k=KT2)
        xs_lo = ring_lo[:, 0:1024].rearrange("p (c k n) -> p c k n", c=C, k=KT2)

        S = pb("S", [P128, 4, 512])
        PR = pb("PR", [P128, 1024])
        OA = pb("OA", [P128, 512])
        MS = pb("MS", [P128, 512])

        s_w0 = [sem("s_w0a"), sem("s_w0b")]
        s_wor = sem("s_wor")
        s_sphi, s_splo = sem("s_sphi"), sem("s_splo")
        s_job = [sem("s_job0"), sem("s_job1")]
        s_jhi, s_jlo = sem("s_jhi"), sem("s_jlo")
        s_cst, s_xin, s_zero, s_tab = (sem(n) for n in ("s_cst", "s_xin", "s_zero", "s_tab"))
        s_xr = [sem("s_xr0"), sem("s_xr1")]
        s_xhs, s_xls = sem("s_xhs"), sem("s_xls")
        s_proj, s_cp, s_mx, s_eq, s_na, s_ea, s_ln = (sem(n) for n in ("s_proj", "s_cp", "s_mx", "s_eq", "s_na", "s_ea", "s_ln"))
        s_re, s_gl, s_rt, s_rp = (sem(n) for n in ("s_re", "s_gl", "s_rt", "s_rp"))
        s_g, s_gc, s_eg, s_qd = (sem(n) for n in ("s_g", "s_gc", "s_eg", "s_qd"))
        s_trq, s_trd, s_trk, s_rqT, s_rql, s_qdT, s_kT = (sem(n) for n in ("s_trq", "s_trd", "s_trk", "s_rqT", "s_rql", "s_qdT", "s_kT"))
        s_sc, s_nm, s_exp, s_rl, s_pn = (sem(n) for n in ("s_sc", "s_nm", "s_exp", "s_rl", "s_pn"))
        s_at, s_am, s_pt, s_wta, s_wtd = (sem(n) for n in ("s_at", "s_am", "s_pt", "s_wta", "s_wtd"))
        s_v, s_o, s_kv, s_kvr, s_U, s_oT, s_oTl, s_op, s_acc = (sem(n) for n in ("s_v", "s_o", "s_kv", "s_kvr", "s_U", "s_oT", "s_oTl", "s_op", "s_acc"))
        s_bn, s_ve, s_rs = ([None] + [sem(f"{n}{i}") for i in (1, 2)] for n in ("s_bn", "s_ve", "s_rs"))
        s_x1, s_x1a = sem("s_x1"), sem("s_x1a")
        s_t1, s_xhi, s_xlo, s_lgt, s_lgs, s_lg = (sem(n) for n in ("s_t1", "s_xhi", "s_xlo", "s_lgt", "s_lgs", "s_lg"))
        s_ro, s_lx, s_pe, s_cb, s_ctt, s_ct = (sem(n) for n in ("s_ro", "s_lx", "s_pe", "s_cb", "s_ctt", "s_ct"))
        s_gu, s_bc, s_sg, s_m, s_h, s_hhi, s_hlo, s_dn = (sem(n) for n in ("s_gu", "s_bc", "s_sg", "s_m", "s_h", "s_hhi", "s_hlo", "s_dn"))
        s_x2, s_xo, s_out, s_dnt = (sem(n) for n in ("s_x2", "s_xo", "s_out", "s_dnt"))

        wv_hi = w_hi[:, :].rearrange("p (v n) -> p v n", v=KV)
        wv_lo = w_lo[:, :].rearrange("p (v n) -> p v n", v=KV)
        jobs = []
        for v in range(1, KV):
            for a in (0, WJOB):
                jobs.append((wqkv[:, v, a:a + WJOB], [(wv_hi[:, v, a:a + WJOB], wv_lo[:, v, a:a + WJOB])]))
        for a in range(H * HID // 2, H * HID, WJOB):
            b = min(a + WJOB, H * HID)
            jobs.append((wo_in[:, a:b], [(wo_hi[:, a:b], wo_lo[:, a:b])]))
        n_attn = len(jobs)
        JOBS_AT = (0, 3, 5, 7, 9)
        assert JOBS_AT[C] == n_attn
        sel_at = [(w_lo[:, FT * KT2 * 2 * P128:], 0), (oT_hi[:, :], 4), (oT_lo[:, :], 8)]

        def ffn_piece(f):
            return (wffn[:, f], [(gu_hi[:, f].rearrange("p k w c -> p (k w c)"), gu_lo[:, f].rearrange("p k w c -> p (k w c)")),
                                 (dn_hi[:, f, :], dn_lo[:, f, :])])

        def sel_piece(i):
            a, b = sel_at[i][1], min(sel_at[i][1] + 4, FT)
            return (csel[:, a * P128:b * P128], [(sel_at[i][0][:, 0:(b - a) * P128], None)])

        def sel_of(f):
            return sel_at[f // 4][0][:, (f % 4) * P128:(f % 4 + 1) * P128]

        gate_job = n_attn
        jobs.append((gate, [(gate_hi[:, :, 0:E], gate_lo[:, :, 0:E])]))
        ffn_job, sel_job = {}, {}
        late_jobs = [("f", f) for f in range(6)] + [("s", 0), ("f", 6), ("f", 7), ("s", 1), ("s", 2)] + [("f", f) for f in range(8, FT)]
        for kind, i in late_jobs:
            (ffn_job if kind == "f" else sel_job)[i] = len(jobs)
            jobs.append(ffn_piece(i) if kind == "f" else sel_piece(i))

        def job_stage(j):
            src = jobs[j][0]
            if len(src.shape) == 3:
                return stage[:, j % 2, 0:src.shape[1] * src.shape[2]].rearrange("p (a b) -> p a b", a=src.shape[1])
            return stage[:, j % 2, 0:src.shape[1]]

        def wq_cols(t, kv, k, a, b):
            v = t[:, :].rearrange("p (v k n) -> p v k n", v=KV, k=KT2)
            if isinstance(kv, int):
                return v[:, kv, k, a:b]
            return v[:, bass.ds(kv, 1), k, a:b].rearrange("p o n -> p (o n)")

        def kv_of(g, c):
            g2 = g + c // C
            return g2 % KV

        def tile_of(g, c):
            return ((g + c // C) // KV) * C + c % C

        def acc_tile(g, c):
            t = tile_of(g, c)
            if isinstance(t, int):
                return acc[:, t, :]
            return acc[:, bass.ds(t, 1), :].rearrange("p o n -> p (o n)")

        block = ctx.enter_context(nc.Block())

        @block.sync
        def _(sp):
            def load_x(g, c):
                u = C * g + c
                later(sp, s_xls, u - 1)
                t = tile_of(g, c)
                cols = slice(t * P128, (t + 1) * P128) if isinstance(t, int) else bass.ds(t * P128, P128)
                sp.dma_start(xraw[:, c % 2, :, :], x_cols.rearrange("(k p) t -> p k t", p=P128)[:, :, cols]).then_inc(s_xr[c % 2], 16)

            def load_job(j):
                later(sp, s_jlo, j - 1)
                sp.dma_start(job_stage(j), jobs[j][0]).then_inc(s_job[j % 2], 16)

            load_x(0, 0)
            for i in range(KT2):
                sp.dma_start(prf[:, i * QKV:(i + 1) * QKV], wqkv[:, 0, i * QKV:(i + 1) * QKV]).then_inc(s_w0[i], 16)
            load_x(0, 1)
            sp.dma_start(cos[:, :, :], rope_cos).then_inc(s_cst, 16)
            sp.dma_start(sin[:, :, :], rope_sin).then_inc(s_cst, 16)
            sp.dma_start(cm[:, :], cmat).then_inc(s_cst, 16)
            sp.dma_start(maskb[:, :, :], cmask).then_inc(s_cst, 16)
            sp.dma_start(wTf, wo_in[:, 0:2048]).then_inc(s_wor, 16)
            load_x(0, 2)
            load_x(0, 3)
            load_job(0)
            load_job(1)
            sp.dma_start(acc[:, :, :], x_rows.rearrange("(t p) n -> p t n", p=P128)).then_inc(s_xin, 16)
            for c in range(C):
                load_x(0, c + 4)
                if c:
                    for j in range(JOBS_AT[c - 1] + 2, JOBS_AT[c] + 2):
                        load_job(j)
            with sp.Fori(1, NG - 1) as g:
                for c in range(C):
                    load_x(g, c + 4)
            for j in range(n_attn, len(jobs)):
                load_job(j)
            ov = out.rearrange("b (t p) n -> p (b t) n", p=P128)
            for n in range(NGRP - 1):
                sp.wait_ge(s_xo, 4 * n + 4)
                sp.dma_start(ov[:, 4 * n:4 * n + 4, :], xo).then_inc(s_out, 16)
            for i in (4 * NGRP - 4, 4 * NGRP - 2):
                sp.wait_ge(s_xo, i + 2)
                sp.dma_start(ov[:, i:i + 2, :], xo[:, i % 4:i % 4 + 2, :]).then_inc(s_out, 16)
            sp.wait_ge(s_out, 16 * (NGRP + 1))

        @block.tensor
        def _(pe):
            def project(g, c, between=None, at=3):
                u = C * g + c
                cc = c % C
                kv = kv_of(g, c)
                pe.wait_ge(s_xls, u + 1)
                later(pe, s_cp, u)
                later(pe, s_rqT, u - 1)
                if c > 2:
                    pe.wait_ge(s_rql, 3 * g + c - 2)
                later(pe, s_qdT, u - 1)
                steps = [(k, x, w) for k in range(KT2) for x, w in ((xs_hi, w_hi), (xs_hi, w_lo), (xs_lo, w_hi))]
                for i, (k, x, w) in enumerate(steps):
                    if between and i == at:
                        between()
                    for a, b in ((0, 512), (512, QKV)):
                        last = pe.matmul(PR[:, a:b], x[:, cc, k, :], wq_cols(w, kv, k, a, b),
                                         start=(i == 0), stop=(i == len(steps) - 1))
                last.then_inc(s_proj, 1)

            def gate_sums(g, c):
                u = C * g + c
                cc = c % C
                pe.wait_ge(s_gl, u + 1)
                later(pe, s_kT, 3 * u)
                if c - 2 < C - 1:
                    later(pe, s_kvr, 3 * g + c - 1)
                pe.matmul(MS[:, 0:128], gmat, gl[:, :], start=True, stop=True)
                pe.matmul(MS[:, 128:130], gl[:, :], halves, start=True, stop=True).then_inc(s_g, 1)

            def turn(g, c, has_next):
                u = C * g + c
                par = c % 2
                pe.wait_ge(s_rp, u + 1)
                if has_next:
                    pe.wait_ge(s_cp, u + 2)
                for h in range(GQ):
                    last = pe.transpose(PR[:, h * 128:(h + 1) * 128], rp[:, par, h * 128:(h + 1) * 128], ident)
                last.then_inc(s_trq, 1)
                pe.wait_ge(s_qd, 5 * (u + 1))
                for h in range(GQ):
                    last = pe.transpose(PR[:, 512 + h * 128:512 + (h + 1) * 128], qd[:, par, h * 128:(h + 1) * 128], ident)
                last.then_inc(s_trd, 1)
                pe.wait_ge(s_gc, u + 1)
                later(pe, s_acc, u - 1)
                pe.transpose(MS[:, 0:128], rp[:, par, 512:640], ident)
                pe.transpose(MS[:, 128:256], qd[:, par, 512:640], ident).then_inc(s_trk, 1)

            def score(g, c):
                u = C * g + c
                n = P128 * (c + 1)
                later(pe, s_wta, 6 * g + tri(c - 1) if c else 6 * g)
                later(pe, s_wtd, u)
                for h in range(GQ):
                    pe.matmul(S[:, h, n - 128:n], maskb[:, 0, :], maskb[:, 1, :], start=True, stop=False, skip_group_check=True)
                pe.wait_ge(s_rqT, u + 1)
                pe.wait_ge(s_kT, 3 * u + 3)
                if c:
                    pe.wait_ge(s_rql, 3 * g + c)
                whole, split = ((rqT, k0T),), ((rq_hi, KT_hi), (rq_hi, KT_lo), (rq_lo, KT_hi))
                for h in range(GQ):
                    steps = split if c else whole
                    for i, (q, k) in enumerate(steps):
                        last = pe.matmul(S[:, h, 0:n], q[:, h * 128:(h + 1) * 128], k[:, 0:n], start=False,
                                         stop=(i == len(steps) - 1), skip_group_check=True)
                    if h % 2:
                        last.then_inc(s_sc, 1)

            def gla_matrix(g, c):
                u = C * g + c
                later(pe, s_oTl, u)
                pe.wait_ge(s_qdT, u + 1)
                pe.matmul(OA[:, :], kdT[:, :], qdT[:, c % 2, :], start=True, stop=True).then_inc(s_at, 1)

            def output(g, c):
                u = C * g + c
                kv = kv_of(g, c)
                pe.wait_ge(s_oTl, u + 1)
                steps = [(h, o, w) for h in range(GQ) for o, w in ((oT_hi, wo_hi), (oT_hi, wo_lo), (oT_lo, wo_hi))]
                for i, (h, o, w) in enumerate(steps):
                    a = (kv * GQ + h) * HID
                    r = w[:, a:a + HID] if isinstance(a, int) else w[:, bass.ds(a, HID)]
                    last = pe.matmul(MS[:, 0:HID], o[:, h * 128:(h + 1) * 128], r, start=(i == 0), stop=(i == len(steps) - 1))
                last.then_inc(s_op, 1)

            def turn_weights(g, c):
                u = C * g + c
                pe.wait_ge(s_pn, 4 * (u + 1))
                for j in range(c + 1):
                    for h in range(GQ):
                        last = pe.transpose(S[:, j, h * 128:(h + 1) * 128], pr[:, h, j * 128:(j + 1) * 128], ident)
                    last.then_inc(s_pt, 1)

            def gather(g, c, has_next, between=None):
                u = C * g + c
                pe.wait_ge(s_am, u + 1)
                if c:
                    pe.wait_ge(s_U, 3 * g + c)
                    pe.matmul(OA[:, :], U[:, :], qdT[:, c % 2, :], start=True, stop=False)
                pe.wait_ge(s_v, u + 1)
                for j in range(c + 1):
                    if between and j == 1:
                        between()
                    if j < c:
                        pe.wait_ge(s_wta, 6 * g + tri(c - 1) + j + 1)
                    else:
                        pe.wait_ge(s_wtd, u + 1)
                    last = pe.matmul(OA[:, :], V[:, j, :], wT[:, j, :], start=(c == 0 and j == 0), stop=(j == c))
                last.then_inc(s_o, 1)
                if c < C - 1:
                    pe.wait_ge(s_kT, 3 * (u + 2))
                    pe.matmul(MS[:, 384:512], qd[:, c % 2, 512:640], V[:, c, :], start=True, stop=True).then_inc(s_kv, 1)

            def step(g, c, first=False, last=False):
                n1, n2 = not (last and c >= 3), not (last and c >= 2)
                score(g, c)
                if c:
                    gla_matrix(g, c)
                if n1 and c != 1:
                    gate_sums(g, c + 1)
                if not n1:
                    turn_x1(0, 0)
                    turn_x1(0, 1)
                if n2:
                    if c == 2 and not last:
                        pe.wait_ge(s_jlo, 2 if first else n_attn)
                    if c == 0:
                        project(g, c + 2, lambda: gla_matrix(g, c), at=2)
                    elif c == 1:
                        project(g, c + 2, lambda: gate_sums(g, c + 1), at=4)
                    else:
                        project(g, c + 2)
                if n1:
                    pe.wait_ge(s_gc, C * g + c + 2)
                else:
                    pe.wait_ge(s_kvr, 3 * NG)
                if not (first and c == 0):
                    output(g - 1 if c == 0 else g, C - 1 if c == 0 else c - 1)
                turn_weights(g, c)
                if n1:
                    turn(g, c + 1, n2)
                else:
                    route(0)
                gather(g, c, n1, None if n1 else lambda: turn_logits(0))

            def side(n, k):
                return PR[:, k * 512:(k + 1) * 512] if n == 0 else OA[:, :]

            def turn_x1(n, k):
                pe.wait_ge(s_x1, 4 * (n + 1))
                if n and k == 0:
                    pe.wait_ge(s_ct, n)
                if n and k == 1:
                    pe.wait_ge(s_xlo, 2 * n + 1)
                for i in range(4):
                    last = pe.transpose(side(n, k)[:, i * 128:(i + 1) * 128], x1s[:, i, k * 128:(k + 1) * 128], ident)
                last.then_inc(s_t1, 1)

            def route(n):
                pe.wait_ge(s_xlo, 2 * n + 2)
                if n == 0:
                    pe.wait_ge(s_jlo, gate_job + 1)
                steps = [(k, w, x) for k in range(KT2) for w, x in ((gate_hi, x1T_hi), (gate_lo, x1T_hi), (gate_hi, x1T_lo))]
                for i, (k, w, x) in enumerate(steps):
                    last = pe.matmul(side(n, 0), w[:, k, :], x[:, n % 2, k, :], start=(i == 0), stop=(i == len(steps) - 1))
                last.then_inc(s_lgt, 1)

            def turn_logits(n):
                pe.wait_ge(s_lgs, n + 1)
                for i in range(4):
                    last = pe.transpose(side(n, 1)[:, i * 128:(i + 1) * 128], lgT[:, i * 128:(i + 1) * 128], ident)
                last.then_inc(s_lg, 1)

            def turn_comb(n):
                pe.wait_ge(s_cb, n + 1)
                for i in range(4):
                    last = pe.transpose(side(n, 0)[:, i * 128:(i + 1) * 128], cmb[:, i, :], ident)
                last.then_inc(s_ctt, 1)

            def gate_up(n, f):
                q0 = FT * n + f
                pe.wait_ge(s_jlo, ffn_job[f] + 1)
                pe.wait_ge(s_xlo, 2 * n + 2)
                later(pe, s_m, q0 - 1)
                steps = [(k, w, x) for k in range(KT2) for w, x in ((gu_hi, x1T_hi), (gu_lo, x1T_hi), (gu_hi, x1T_lo))]
                for q in range(2):
                    for i, (k, w, x) in enumerate(steps):
                        last = pe.matmul(S[:, 2 * q + q0 % 2, :], w[:, f, k, q, :], x[:, n % 2, k, :],
                                         start=(i == 0), stop=(i == len(steps) - 1))
                    last.then_inc(s_gu, 1)

            def spread_comb(n, f):
                pe.wait_ge(s_ct, n + 1)
                later(pe, s_h, FT * n + f)
                pe.wait_ge(s_jlo, sel_job[f // 4] + 1)
                pe.matmul(MS[:, :], sel_of(f), combT, start=True, stop=True).then_inc(s_bc, 1)

            def down(n, f):
                q0 = FT * n + f
                pe.wait_ge(s_hhi, q0 + 1)
                pe.wait_ge(s_hlo, q0 + 1)
                if f == 0:
                    later(pe, s_x2, n)
                for i in range(4):
                    t = slice(i * 128, (i + 1) * 128)
                    for j, (hh, w) in enumerate(((hT_hi, dn_hi), (hT_hi, dn_lo), (hT_lo, dn_hi))):
                        last = pe.matmul(PR[:, i * 256:(i + 1) * 256], hh[:, q0 % 2, t], w[:, f, :],
                                         start=(f == 0 and j == 0 and i % 2 == 0), stop=(f == FT - 1 and j == 2),
                                         skip_group_check=True)
                    if q0 == FT * NGRP - 1:
                        last.then_inc(s_dnt, 1)
                if q0 < FT * NGRP - 1:
                    last.then_inc(s_dn, 1)

            pe.wait_ge(s_splo, 1)
            project(0, 0, lambda: pe.wait_ge(s_splo, 2))
            pe.wait_ge(s_cst, 64)
            project(0, 1)
            gate_sums(0, 0)
            turn(0, 0, True)
            for c in range(C):
                if c == 1:
                    pe.wait_ge(s_splo, 3)
                step(0, c, first=True)
            pe.wait_ge(s_splo, 4)
            with pe.Fori(1, NG - 1) as g:
                for c in range(C):
                    step(g, c)
            for c in range(C):
                step(NG - 1, c, last=True)
            gate_up(0, 0)
            turn_comb(0)
            pe.wait_ge(s_acc, NU - 1)
            output(NG - 1, C - 1)
            gate_up(0, 1)
            pe.wait_ge(s_acc, NU)
            for n in range(NGRP):
                for f in range(FT):
                    if n or f > 1:
                        gate_up(n, f)
                    end = n == NGRP - 1 and f == FT - 1
                    if end:
                        spread_comb(n, f)
                    if n == 0 and f == 2:
                        spread_comb(0, 1)
                    if n or f > 1:
                        down(n if f > 1 else n - 1, (f - 2) % FT)
                    if not end and (n or f != 1):
                        spread_comb(n, f)
                    if n < NGRP - 1:
                        if f == 4:
                            turn_x1(n + 1, 0)
                        if f == 5:
                            turn_x1(n + 1, 1)
                        if f == 6:
                            route(n + 1)
                        if f == 7:
                            turn_logits(n + 1)
                        if f == 10:
                            turn_comb(n + 1)
            down(NGRP - 1, FT - 2)
            down(NGRP - 1, FT - 1)

        @block.scalar
        def _(act):
            def o_out(g, c):
                u = C * g + c
                act.wait_ge(s_o, u + 1)
                later(act, s_op, u)
                nc.scalar.copy(oT_hi[:, :], OA[:, :]).then_inc(s_oT, 1)

            def exps(g, c):
                u = C * g + c
                n = P128 * (c + 1)
                later(act, s_pt, 10 * g + tri(c))
                for h in range(GQ):
                    if h % 2 == 0:
                        act.wait_ge(s_nm, 2 * u + 1 + h // 2)
                    nc.scalar.activation(pr[:, h, 0:n], S[:, h, 0:n], ACT.Exp, bias=nm[:, h:h + 1], scale=1.0,
                                         accum_out=ls[:, h:h + 1]).then_inc(s_exp, 1)

            def exp_gates(g, c):
                u = C * g + c
                w = P128 + 2
                act.wait_ge(s_gc, u + 1)
                par = c % 2
                nc.scalar.activation(eg[:, par, 0:w], gc[:, 0:w], ACT.Exp, scale=1.0 / GATE_NORM).then_inc(s_eg, 1)
                nc.scalar.activation(eg[:, par, 130:258], gc[:, 0:128], ACT.Exp, scale=-1.0 / GATE_NORM).then_inc(s_eg, 1)

            def copy_out(g, c):
                u = C * g + c
                act.wait_ge(s_proj, u + 1)
                later(act, s_v, u - 3)
                nc.scalar.copy(qkv[:, c % C, :], PR[:, 0:QKV]).then_inc(s_cp, 1)

            def features(g, c):
                u = C * g + c
                par = c % 2
                act.wait_ge(s_mx, u + 1)
                later(act, s_qd, 5 * (u - 1))
                later(act, s_re, u)
                for h in range(GQ + 1):
                    last = nc.scalar.activation(eqk[:, par, h * 128:(h + 1) * 128], qkv[:, c % C, h * 128:(h + 1) * 128],
                                                ACT.Exp, bias=nmx[:, h:h + 1], scale=1.0, accum_out=se[:, h:h + 1])
                last.then_inc(s_eq, 1)

            def gate_logs(g, c):
                u = C * g + c
                act.wait_ge(s_na, u + 1)
                nc.scalar.activation(eabs[:, :], nabs[:, :], ACT.Exp).then_inc(s_ea, 1)
                act.wait_ge(s_ea, u + 1)
                later(act, s_gl, u)
                nc.scalar.activation(lnp[:, :], eabs[:, :], ACT.Ln, bias=1.0).then_inc(s_ln, 1)

            def weights_out(g, c):
                u = C * g + c
                later(act, s_o, u)
                for j in range(c):
                    act.wait_ge(s_pt, 10 * g + tri(c) + j + 1)
                    nc.scalar.copy(wT[:, j, :], S[:, j, :]).then_inc(s_wta, 1)

            def q_out(g, c):
                u = C * g + c
                act.wait_ge(s_trq, u + 1)
                later(act, s_sc, 2 * u)
                nc.scalar.copy(rq_hi[:, :] if c % C else rqT[:, :], PR[:, 0:512]).then_inc(s_rqT, 1)

            def qd_out(g, c):
                u = C * g + c
                act.wait_ge(s_trd, u + 1)
                later(act, s_o, u - 1)
                nc.scalar.copy(qdT[:, c % 2, :], PR[:, 512:1024]).then_inc(s_qdT, 1)

            def step(g, c, first=False, last=False):
                n1, n2 = not (last and c >= 3), not (last and c >= 2)
                if c != 1 and not (first and c == 0):
                    o_out(g - 1 if c == 0 else g, C - 1 if c == 0 else c - 1)
                exps(g, c)
                if n1:
                    exp_gates(g, c + 1)
                if n2:
                    copy_out(g, c + 2)
                if not n1:
                    x1_hi(0, 0)
                    x1_hi(0, 1)
                if first and c:
                    act.wait_ge(s_splo, 3 if c == 1 else 4)
                weights_out(g, c)
                if n1:
                    q_out(g, c + 1)
                    qd_out(g, c + 1)
                if c == 0:
                    o_out(g, c)
                if n2:
                    features(g, c + 2)
                    gate_logs(g, c + 2)

            def side(n, k):
                return PR[:, k * 512:(k + 1) * 512] if n == 0 else OA[:, :]

            def x1_hi(n, k):
                act.wait_ge(s_t1, 2 * n + k + 1)
                nc.scalar.copy(x1T_hi[:, n % 2, k, :], side(n, k)).then_inc(s_xhi, 1)

            def logits_out(n):
                act.wait_ge(s_lgt, n + 1)
                nc.scalar.copy(lgT, side(n, 0)).then_inc(s_lgs, 1)

            def router_exp(n):
                act.wait_ge(s_lx, n + 1)
                nc.scalar.activation(pe_[:, :, :], lx[:, :, :], ACT.Exp).then_inc(s_pe, 1)

            def comb_out(n):
                act.wait_ge(s_ctt, n + 1)
                later(act, s_bc, FT * n)
                nc.scalar.copy(combT, side(n, 0)).then_inc(s_ct, 1)

            def silu(n, f):
                q0 = FT * n + f
                act.wait_ge(s_gu, 2 * q0 + 2)
                later(act, s_m, q0 - 1)
                nc.scalar.activation(sg[:, q0 % 2, :], S[:, q0 % 2, :], ACT.Silu).then_inc(s_sg, 1)

            def h_hi(n, f):
                q0 = FT * n + f
                act.wait_ge(s_h, q0 + 1)
                later(act, s_dn, q0 - 1)
                nc.scalar.copy(hT_hi[:, q0 % 2, :], hbuf[:, q0 % 2, :]).then_inc(s_hhi, 1)

            def wo_high(i):
                a = slice(i * 1024, (i + 1) * 1024)
                nc.scalar.copy(wo_hi[:, a], wTf[:, a]).then_inc(s_sphi, 1)

            act.preload_act_table_set("natural_log_exp_and_others")
            for i in range(KT2):
                act.wait_ge(s_w0[i], 16)
                nc.scalar.copy(w_hi[:, i * QKV:(i + 1) * QKV], prf[:, i * QKV:(i + 1) * QKV]).then_inc(s_sphi, 1)
            copy_out(0, 0)
            features(0, 0)
            gate_logs(0, 0)
            copy_out(0, 1)
            exp_gates(0, 0)
            q_out(0, 0)
            features(0, 1)
            qd_out(0, 0)
            gate_logs(0, 1)
            act.wait_ge(s_wor, 16)
            wo_high(0)
            for c in range(C):
                step(0, c, first=True)
                if c == 0:
                    wo_high(1)
            with act.Fori(1, NG - 1) as g:
                for c in range(C):
                    step(g, c)
            for c in range(C):
                step(NG - 1, c, last=True)
            logits_out(0)
            router_exp(0)
            o_out(NG - 1, C - 1)
            silu(0, 0)
            comb_out(0)
            for n in range(NGRP):
                for f in range(FT):
                    if n or f:
                        silu(n, f)
                    h_hi(n, f)
                    if n < NGRP - 1:
                        if f == 4:
                            x1_hi(n + 1, 0)
                        if f == 5:
                            x1_hi(n + 1, 1)
                        if f == 6:
                            logits_out(n + 1)
                        if f == 7:
                            router_exp(n + 1)
                        if f == 10:
                            comb_out(n + 1)

        @block.vector
        def _(dve):
            def exp_view(t):
                return t.rearrange("p (h d) -> p h d", d=128)

            def move_v(g, c):
                u = C * g + c
                later(dve, s_o, u)
                nc.vector.tensor_copy(V[:, c, :], qkv[:, c, 640:768]).then_inc(s_v, 1)

            def o_low(g, c):
                dve.wait_ge(s_oT, C * g + c + 1)
                nc.vector.tensor_tensor(oT_lo[:, :], OA[:, :], oT_hi[:, :].bitcast(F32), ALU.subtract).then_inc(s_oTl, 1)

            def score_max(g, c, pair):
                u = C * g + c
                n = P128 * (c + 1)
                dve.wait_ge(s_sc, 2 * u + 1 + pair)
                later(dve, s_exp, 4 * u)
                nc.vector.tensor_reduce(nm[:, 2 * pair:2 * pair + 2], S[:, 2 * pair:2 * pair + 2, 0:n], AX_X, ALU.max,
                                        negate=True).then_inc(s_nm, 1)

            def mask_gla(g, c):
                u = C * g + c
                dve.wait_ge(s_at, u + 1)
                nc.vector.tensor_tensor(exp_view(am[:, :]), exp_view(OA[:, :]),
                                        keep.rearrange("p (o t) -> p o t", o=1).to_broadcast([P128, GQ, P128]),
                                        ALU.mult).then_inc(s_am, 1)

            def update_state(g, c):
                u = C * g + c
                dve.wait_ge(s_kv, 3 * g + c)
                dve.wait_ge(s_eg, 2 * (u + 1))
                if c == 1:
                    nc.vector.tensor_copy(Ut[:, :], MS[:, 384:512]).then_inc(s_kvr, 1)
                else:
                    nc.vector.tensor_tensor(Ut[:, :], MS[:, 384:512], U[:, :], ALU.add).then_inc(s_kvr, 1)
                dve.wait_ge(s_kvr, 3 * g + c)
                later(dve, s_o, u)
                nc.vector.tensor_scalar(U[:, :], Ut[:, :], eg[:, 1 - c % 2, 129:130], eg[:, c % 2, 128:129],
                                        ALU.mult, ALU.mult).then_inc(s_U, 1)

            def normalise(g, c, pair):
                u = C * g + c
                n = P128 * (c + 1)
                dve.wait_ge(s_exp, 4 * u + 2 * pair + 2)
                nc.vector.reciprocal(rl[:, 2 * pair:2 * pair + 2], ls[:, 2 * pair:2 * pair + 2]).then_inc(s_rl, 1)
                dve.wait_ge(s_rl, 2 * u + pair + 1)
                for h in (2 * pair, 2 * pair + 1):
                    nc.vector.tensor_scalar(pr[:, h, 0:n], pr[:, h, 0:n], rl[:, h:h + 1], None, ALU.mult).then_inc(s_pn, 1)

            def clamp_gates(g, c):
                u = C * g + c
                w = P128 + 2
                dve.wait_ge(s_g, u + 1)
                later(dve, s_eg, 2 * u)
                nc.vector.tensor_scalar(gc[:, 0:w], MS[:, 0:w], -GCLAMP, GCLAMP, ALU.max, ALU.min).then_inc(s_gc, 1)

            def decay(g, c):
                u = C * g + c
                par = c % 2
                dve.wait_ge(s_eg, 2 * (u + 1))
                dve.wait_ge(s_re, u + 1)
                later(dve, s_trk, u - 1)
                if (c - 2) % C < C - 1:
                    later(dve, s_kv, kv_count(g, c - 2))
                for h in range(GQ + 1):
                    e = eg[:, par, 0:128] if h < GQ else eg[:, par, 130:258]
                    nc.vector.scalar_tensor_tensor(out=qd[:, par, h * 128:(h + 1) * 128], in0=eqk[:, par, h * 128:(h + 1) * 128],
                                                   scalar=rse[:, par, h:h + 1], in1=e, op0=ALU.mult,
                                                   op1=ALU.mult).then_inc(s_qd, 1)

            def kv_count(g, c):
                return 3 * g + c + 1 if c >= 0 else 3 * g + min(c + 1, 0)

            def add_output(g, c):
                u = C * g + c
                dve.wait_ge(s_op, u + 1)
                a = acc_tile(g, c)
                nc.vector.scalar_tensor_tensor(out=a, in0=MS[:, 0:HID], scalar=0.5, in1=a, op0=ALU.mult,
                                               op1=ALU.add).then_inc(s_acc, 1)

            def prepare(g, c):
                u = C * g + c
                x = qkv[:, c % C, 0:QK]
                dve.wait_ge(s_cp, u + 1)
                later(dve, s_eq, u)
                nc.vector.tensor_reduce(nmx[:, :], exp_view(x), AX_X, ALU.max, negate=True).then_inc(s_mx, 1)
                later(dve, s_ea, u)
                k = qkv[:, c % C, 512:640]
                nc.vector.scalar_tensor_tensor(out=nabs[:, :], in0=k, scalar=-1.0, in1=k, op0=ALU.mult,
                                               op1=ALU.min).then_inc(s_na, 1)

            def add_gla(g, c):
                u = C * g + c
                dve.wait_ge(s_pt, 10 * g + tri(c) + c + 1)
                dve.wait_ge(s_am, u + 1)
                later(dve, s_o, u)
                nc.vector.tensor_tensor(wT[:, c, :], S[:, c, :], am[:, :], ALU.add).then_inc(s_wtd, 1)

            def wo_low(i):
                dve.wait_ge(s_sphi, i + 3)
                a = slice(i * 1024, (i + 1) * 1024)
                nc.vector.tensor_tensor(wo_lo[:, a], wTf[:, a], wo_hi[:, a].bitcast(F32), ALU.subtract).then_inc(s_splo, 1)

            def k_out(g, c):
                u = C * g + c
                dve.wait_ge(s_trk, u + 1)
                later(dve, s_sc, 2 * u)
                later(dve, s_at, u)
                a = slice((c % C) * 128, (c % C + 1) * 128)
                if c % C == 0:
                    nc.vector.tensor_copy(k0T[:, :], MS[:, 0:128])
                nc.vector.tensor_copy(KT_hi[:, a], MS[:, 0:128]).then_inc(s_kT, 1)
                nc.vector.tensor_copy(kdT[:, :], MS[:, 128:256]).then_inc(s_kT, 1)
                dve.wait_ge(s_kT, 3 * u + 1)
                nc.vector.tensor_tensor(KT_lo[:, a], MS[:, 0:128], KT_hi[:, a].bitcast(F32), ALU.subtract).then_inc(s_kT, 1)

            def q_low(g, c):
                u = C * g + c
                if c % C:
                    dve.wait_ge(s_rqT, u + 1)
                    nc.vector.tensor_tensor(rq_lo[:, :], PR[:, 0:512], rq_hi[:, :].bitcast(F32), ALU.subtract).then_inc(s_rql, 1)

            def log_gates(g, c):
                u = C * g + c
                par = c % 2
                dve.wait_ge(s_eq, u + 1)
                later(dve, s_qd, 5 * (u - 1))
                nc.vector.reciprocal(rse[:, par, :], se[:, :]).then_inc(s_re, 1)
                dve.wait_ge(s_ln, u + 1)
                later(dve, s_g, u)
                nc.vector.scalar_tensor_tensor(out=gl[:, :], in0=qkv[:, c % C, 512:640], scalar=0.0, in1=lnp[:, :],
                                               op0=ALU.min, op1=ALU.subtract).then_inc(s_gl, 1)

            def step(g, c, first=False, last=False):
                n1, n2 = not (last and c >= 3), not (last and c >= 2)
                if c > 1:
                    o_low(g, c - 1)
                if c:
                    update_state(g, c)
                score_max(g, c, 0)
                if c == 0 and not first:
                    o_low(g - 1, C - 1)
                score_max(g, c, 1)
                if c == 1:
                    log_gates(g, c + 1)
                if c:
                    mask_gla(g, c)
                if n1 and c == 1:
                    clamp_gates(g, c + 1)
                normalise(g, c, 0)
                move_v(g, c)
                if n1 and c != 1:
                    clamp_gates(g, c + 1)
                normalise(g, c, 1)
                if c == 0:
                    mask_gla(g, c)
                if n1:
                    decay(g, c + 1)
                else:
                    x1_lo(0, 0)
                    x1_lo(0, 1)
                if first and c == 0:
                    wo_low(0)
                else:
                    add_output(g - 1 if c == 0 else g, C - 1 if c == 0 else c - 1)
                if n2 and c:
                    prepare(g, c + 2)
                if last and c == 1:
                    norm_stats(1, 0)
                    norm_aggr(1, 0)
                if last and c == 2:
                    norm1(0)
                if first and c in (0, 2):
                    dve.wait_ge(s_splo, 4 if c else 3)
                add_gla(g, c)
                if n1:
                    k_out(g, c + 1)
                    q_low(g, c + 1)
                if c == 0:
                    prepare(g, c + 2)
                    o_low(g, c)
                if n2 and c:
                    log_gates(g, c + 2)
                if first and c == 1:
                    wo_low(1)

            def side(n, k):
                return PR[:, k * 512:(k + 1) * 512] if n == 0 else OA[:, :]

            def norm_stats(which, n):
                for i in range(4):
                    nc.vector.bn_stats(st[which][:, i, :], acc[:, 4 * n + i, :] if which == 1 else x2[:, i, :]).then_inc(s_bn[which], 1)

            def norm_aggr(which, n):
                dve.wait_ge(s_bn[which], 8 * n + 4)
                if which == 1:
                    later(dve, s_x1a, 4 * n)
                for i in range(4):
                    nc.vector.bn_aggr(mv[which][:, i, :], st[which][:, i, :]).then_inc(s_bn[which], 1)
                dve.wait_ge(s_bn[which], 8 * n + 8)
                nc.vector.tensor_scalar(ve[which][:, :], mv[which][:, :, 1], EPS, None, ALU.add).then_inc(s_ve[which], 1)

            def norm1(n):
                dve.wait_ge(s_rs[1], n + 1)
                later(dve, s_t1, 2 * n)
                for i in range(4):
                    nc.vector.tensor_scalar(x1s[:, i, :], acc[:, 4 * n + i, :], mv[1][:, i, 0:1], rstd[1][:, i:i + 1],
                                            ALU.subtract, ALU.mult).then_inc(s_x1, 1)

            def x1_lo(n, k):
                dve.wait_ge(s_xhi, 2 * n + k + 1)
                nc.vector.tensor_tensor(x1T_lo[:, n % 2, k, :], side(n, k), x1T_hi[:, n % 2, k, :].bitcast(F32),
                                        ALU.subtract).then_inc(s_xlo, 1)

            routed = [0]

            def link(ins):
                routed[0] += 1
                ins.then_inc(s_ro, 1)
                dve.wait_ge(s_ro, routed[0])

            def route_rank(n):

                dve.wait_ge(s_lg, n + 1)
                link(nc.vector.tensor_copy(lg[:, :, :], side(n, 1).rearrange("p (a n) -> p a n", a=4)[:, :, 0:E]))
                link(nc.vector.tensor_reduce(small[:, 0:4], lg[:, :, :], AX_X, ALU.max))
                nc.vector.tensor_tensor(lx[:, :, :], lg[:, :, :], small[:, 0:4].rearrange("p (a o) -> p a o", o=1)
                                        .to_broadcast([P128, 4, E]), ALU.subtract).then_inc(s_lx, 1)
                me = lg[:, :, :].rearrange("p a (e o) -> p a e o", o=1).to_broadcast([P128, 4, E, E])
                you = lg[:, :, :].rearrange("p a (o e) -> p a o e", o=1).to_broadcast([P128, 4, E, E])
                r1 = rk1[:, :].rearrange("p (a e f) -> p a e f", a=4, e=E)
                r2 = rk2[:, :].rearrange("p (a e f) -> p a e f", a=4, e=E)
                link(nc.vector.tensor_tensor(r1, you, me, ALU.is_gt))
                link(nc.vector.tensor_tensor(r2, you, me, ALU.is_equal))
                link(nc.vector.tensor_tensor(r2, r2, tri8[:, :, :].rearrange("p (o e) f -> p o e f", o=1)
                                             .to_broadcast([P128, 4, E, E]), ALU.mult))
                link(nc.vector.tensor_tensor(rk1[:, :], rk1[:, :], rk2[:, :], ALU.add))
                link(nc.vector.tensor_reduce(rank[:, :, :], r1, AX_X, ALU.add))
                link(nc.vector.tensor_scalar(topm[:, :, :], rank[:, :, :], 2.0, None, ALU.is_lt))

            def route_weigh(n):
                dve.wait_ge(s_pe, n + 1)
                link(nc.vector.tensor_reduce(small[:, 4:8], pe_[:, :, :], AX_X, ALU.add))
                link(nc.vector.reciprocal(small[:, 8:12], small[:, 4:8]))
                link(nc.vector.tensor_tensor(comb[:, :, :], pe_[:, :, :], topm[:, :, :], ALU.mult))
                link(nc.vector.tensor_tensor(comb[:, :, :], comb[:, :, :], small[:, 8:12]
                                             .rearrange("p (a o) -> p a o", o=1).to_broadcast([P128, 4, E]), ALU.mult))
                link(nc.vector.tensor_copy(cmb[:, :, 0:E].bitcast(F32R), comb[:, :, :]))
                nc.vector.tensor_tensor(cmb[:, :, E:2 * E], comb[:, :, :], cmb[:, :, 0:E], ALU.subtract).then_inc(s_cb, 1)

            def multiply(n, f):
                q0 = FT * n + f
                dve.wait_ge(s_sg, q0 + 1)
                nc.vector.tensor_tensor(am[:, :], sg[:, q0 % 2, :], S[:, 2 + q0 % 2, :], ALU.mult).then_inc(s_m, 1)
                if n and f == 1:
                    add_ffn(n - 1)
                dve.wait_ge(s_m, q0 + 1)
                dve.wait_ge(s_bc, q0 + 1)
                later(dve, s_hhi, q0 - 1)
                nc.vector.tensor_tensor(hbuf[:, q0 % 2, :], am[:, :], MS[:, :], ALU.mult).then_inc(s_h, 1)

            def h_lo(n, f):
                q0 = FT * n + f
                dve.wait_ge(s_hhi, q0 + 1)
                later(dve, s_dn, q0 - 1)
                nc.vector.tensor_tensor(hT_lo[:, q0 % 2, :], hbuf[:, q0 % 2, :], hT_hi[:, q0 % 2, :].bitcast(F32),
                                        ALU.subtract).then_inc(s_hlo, 1)

            def add_ffn(n):
                dve.wait_ge(s_dn, FT * (n + 1))
                dve.wait_ge(s_x1a, 4 * n + 4)
                nc.vector.tensor_tensor(x2.rearrange("p a n -> p (a n)"), PR[:, :],
                                        acc[:, 4 * n:4 * n + 4, :].rearrange("p a n -> p (a n)"), ALU.add).then_inc(s_x2, 1)

            def norm2(n):
                dve.wait_ge(s_rs[2], n + 1)
                later(dve, s_out, 16 * n)
                for i in range(4):
                    nc.vector.tensor_scalar(xo[:, i, :], x2[:, i, :], mv[2][:, i, 0:1], rstd[2][:, i:i + 1],
                                            ALU.subtract, ALU.mult).then_inc(s_xo, 1)

            def finish_half(k):
                dve.wait_ge(s_rs[2], NGRP + k)
                for i in (2 * k, 2 * k + 1):
                    nc.vector.tensor_scalar(xo[:, i, :], x2[:, i, :], mv[2][:, i, 0:1], rstd[2][:, i:i + 1],
                                            ALU.subtract, ALU.mult).then_inc(s_xo, 1)

            nc.vector.memset(gate_hi[:, :, :].bitcast(F32), 0.0).then_inc(s_zero, 1)
            nc.vector.memset(gate_lo[:, :, :].bitcast(F32), 0.0).then_inc(s_zero, 1)
            for i in range(KT2):
                dve.wait_ge(s_sphi, i + 1)
                a = slice(i * QKV, (i + 1) * QKV)
                nc.vector.tensor_tensor(w_lo[:, a], prf[:, a], w_hi[:, a].bitcast(F32), ALU.subtract).then_inc(s_splo, 1)
            dve.wait_ge(s_cst, 64)
            prepare(0, 0)
            log_gates(0, 0)
            clamp_gates(0, 0)
            prepare(0, 1)
            decay(0, 0)
            k_out(0, 0)
            log_gates(0, 1)
            dve.wait_ge(s_xin, 16)
            for c in range(C):
                step(0, c, first=True)
            with dve.Fori(1, NG - 1) as g:
                for c in range(C):
                    step(g, c)
            for c in range(C):
                step(NG - 1, c, last=True)
            nc.vector.memset(rqT[:, :], 0.0).then_inc(s_zero, 1)
            dve.wait_ge(s_zero, 3)
            dve.wait_ge(s_tab, 2)
            route_rank(0)
            route_weigh(0)
            o_low(NG - 1, C - 1)
            add_output(NG - 1, C - 1)
            for n in range(NGRP):
                for f in range(FT):
                    multiply(n, f)
                    h_lo(n, f)
                    if n:
                        if f == 2:
                            dve.wait_ge(s_x2, n)
                            norm_stats(2, n - 1)
                        if f == 4:
                            norm_aggr(2, n - 1)
                        if f == 6:
                            norm2(n - 1)
                    if n < NGRP - 1:
                        if f == 0:
                            norm_stats(1, n + 1)
                        if f == 1:
                            norm_aggr(1, n + 1)
                        if f == 3:
                            norm1(n + 1)
                        if f == 4:
                            x1_lo(n + 1, 0)
                        if f == 5:
                            x1_lo(n + 1, 1)
                        if f == 7:
                            route_rank(n + 1)
                        if f == 8:
                            route_weigh(n + 1)
            n = NGRP - 1
            dve.wait_ge(s_x1a, 4 * n + 4)
            dve.wait_ge(s_out, 16 * n)
            for k in range(2):
                dve.wait_ge(s_dnt, 2 * k + 2)
                nc.vector.tensor_tensor(x2[:, 2 * k:2 * k + 2, :].rearrange("p a n -> p (a n)"), PR[:, 512 * k:512 * k + 512],
                                        acc[:, 4 * n + 2 * k:4 * n + 2 * k + 2, :].rearrange("p a n -> p (a n)"),
                                        ALU.add).then_inc(s_x2, 1)
                dve.wait_ge(s_x2, n + k + 1)
                for i in (2 * k, 2 * k + 1):
                    nc.vector.bn_stats(st[2][:, i, :], x2[:, i, :]).then_inc(s_bn[2], 1)
                if k:
                    finish_half(0)
                dve.wait_ge(s_bn[2], 8 * n + 4 * k + 2)
                for i in (2 * k, 2 * k + 1):
                    nc.vector.bn_aggr(mv[2][:, i, :], st[2][:, i, :]).then_inc(s_bn[2], 1)
                dve.wait_ge(s_bn[2], 8 * n + 4 * k + 4)
                nc.vector.tensor_scalar(ve[2][:, 2 * k:2 * k + 2], mv[2][:, 2 * k:2 * k + 2, 1], EPS, None,
                                        ALU.add).then_inc(s_ve[2], 1)
            finish_half(1)

        @block.gpsimd
        def _(pool):
            def rotate(g, c):
                u = C * g + c
                x4 = qkv[:, c % C, 0:QK].rearrange("p (h w d) -> p h w d", w=2, d=64)
                pool.wait_ge(s_cp, u + 1)
                later(pool, s_rp, u)
                later(pool, s_trk, u - 1)
                for t, src, to in ((cos, x4, rp[:, c % 2, :]), (sin, x4[:, :, ::-1, :], rt[:, :])):
                    tab = t[:, c % C, :].rearrange("p (o w d) -> p o w d", o=1, w=2).to_broadcast([P128, GQ + 1, 2, 64])
                    nc.gpsimd.tensor_tensor(to.rearrange("p (h w d) -> p h w d", w=2, d=64), src, tab,
                                            ALU.mult).then_inc(s_rt, 1)
                pool.wait_ge(s_rt, 2 * (u + 1))
                nc.gpsimd.tensor_tensor(rp[:, c % 2, :], rp[:, c % 2, :], rt[:, :], ALU.add).then_inc(s_rp, 1)

            def x_wait(g, c):
                u = C * g + c
                pool.wait_ge(s_xr[c % 2], 16 * (2 * g + c // 2 + 1))
                later(pool, s_proj, u - 3)

            def x_split(g, c):
                u = C * g + c
                hi, lo, raw = xs_hi[:, c % C, :, :], xs_lo[:, c % C, :, :], xraw[:, c % 2, :, :]
                nc.gpsimd.tensor_scalar(hi, raw, 1.0, 0.0, ALU.mult, ALU.add).then_inc(s_xhs, 1)
                pool.wait_ge(s_xhs, u + 1)
                nc.gpsimd.tensor_tensor(lo, raw, hi.bitcast(F32), ALU.subtract).then_inc(s_xls, 1)

            def split(j):
                pool.wait_ge(s_job[j % 2], 16 * (j // 2 + 1))
                at = 0
                for i, (hi, lo) in enumerate(jobs[j][1]):
                    n = hi.shape[-1] * (hi.shape[1] if len(hi.shape) == 3 else 1)
                    raw = stage[:, j % 2, at:at + n]
                    if len(hi.shape) == 3:
                        raw = raw.rearrange("p (a b) -> p a b", a=hi.shape[1])
                    at += n
                    nc.gpsimd.tensor_scalar(hi, raw, 1.0, 0.0, ALU.mult, ALU.add).then_inc(s_jhi, 1)
                    jh[0] += 1
                    if lo is None:
                        pool.wait_ge(s_jhi, jh[0])
                        nc.gpsimd.engine_nop().then_inc(s_jlo, 1)
                        return
                    pool.wait_ge(s_jhi, jh[0])
                    last = nc.gpsimd.tensor_tensor(lo, raw, hi.bitcast(F32), ALU.subtract)
                last.then_inc(s_jlo, 1)

            jh = [0]

            def step(g, c, last=False):
                if not last:
                    x_wait(g, c + 4)
                if not (last and c >= 2):
                    rotate(g, c + 2)
                if not last:
                    x_split(g, c + 4)

            def keep_norm1(n):
                pool.wait_ge(s_x1, 4 * n + 4)
                for i in range(4):
                    a = acc[:, 4 * n + i, :]
                    nc.gpsimd.tensor_scalar(a, a, mv[1][:, i, 0:1], rstd[1][:, i:i + 1],
                                            ALU.subtract, ALU.mult).then_inc(s_x1a, 1)

            def rs(which, n):
                pool.wait_ge(s_ve[which], n + 1)
                nc.gpsimd.tensor_tensor(rstd[which][:, :], ve[which][:, :], neghalf[:, :], ALU.pow).then_inc(s_rs[which], 1)

            for c in range(3):
                x_wait(0, c)
                x_split(0, c)
            nc.gpsimd.memset(neghalf[:, :], -0.5).then_inc(s_tab, 1)
            for e in range(E):
                if e:
                    nc.gpsimd.memset(tri8[:, e, 0:e], 1.0)
                last = nc.gpsimd.memset(tri8[:, e, e:E], 0.0)
            last.then_inc(s_tab, 1)
            pool.wait_ge(s_cst, 64)
            rotate(0, 0)
            rotate(0, 1)
            x_wait(0, 3)
            x_split(0, 3)
            pool.wait_ge(s_zero, 2)
            for c in range(C):
                step(0, c)
                for j in range(JOBS_AT[c], JOBS_AT[c + 1]):
                    split(j)
            with pool.Fori(1, NG - 1) as g:
                for c in range(C):
                    step(g, c)
            for c in range(C):
                step(NG - 1, c, last=True)
                if c == 0:
                    split(gate_job)
                if c == 1:
                    rs(1, 0)
                if c == 3:
                    keep_norm1(0)
                for kind, i in late_jobs[3 * c:3 * c + 3] if c < C - 1 else late_jobs[3 * c:]:
                    if kind == "s":
                        pool.wait_ge(s_proj, NU)
                        if i:
                            pool.wait_ge(s_op, NU)
                        split(sel_job[i])
                    else:
                        pool.wait_ge(s_proj, NU - C if i < 9 else NU)
                        pool.wait_ge(s_op, NU - 2 * C if i < 8 else NU - C)
                        split(ffn_job[i])
            for n in range(NGRP):
                if n < NGRP - 1:
                    rs(1, n + 1)
                    keep_norm1(n + 1)
                if n:
                    rs(2, n - 1)
            for k in range(2):
                h = slice(2 * k, 2 * k + 2)
                pool.wait_ge(s_ve[2], NGRP + k)
                nc.gpsimd.tensor_tensor(rstd[2][:, h], ve[2][:, h], neghalf[:, h], ALU.pow).then_inc(s_rs[2], 1)


def kernel(L0_attn_hidden_states, L0_attn_Wq, L0_attn_Wk, L0_attn_Wv, L0_attn_Wo, L0_ffn_gate_w, L0_ffn_w_gate,
           L0_ffn_w_up, L0_ffn_w_down):
    import numpy as np
    import concourse.bacc as bacc
    from concourse.bass_utils import run_bass_kernel_spmd

    x = np.ascontiguousarray(L0_attn_hidden_states).reshape(B * N, HID)

    def by_kv(w, heads):
        return w.reshape(KT2, P128, KV, heads * D).transpose(1, 2, 0, 3)

    wqkv = np.concatenate([by_kv(np.asarray(L0_attn_Wq), GQ), by_kv(np.asarray(L0_attn_Wk), 1),
                           by_kv(np.asarray(L0_attn_Wv), 1)], axis=3)
    wo = np.asarray(L0_attn_Wo).reshape(H, D, HID).transpose(1, 0, 2)

    def features(w):
        return np.asarray(w).transpose(1, 0, 2).reshape(KT2, P128, FT, P128).transpose(1, 2, 0, 3)

    wgu = np.stack([features(L0_ffn_w_gate), features(L0_ffn_w_up)], axis=3)
    wdn = np.asarray(L0_ffn_w_down).reshape(FT, P128, HID).transpose(1, 0, 2)
    gate = np.asarray(L0_ffn_gate_w).T.reshape(KT2, P128, E).transpose(1, 0, 2)

    f32 = np.float32
    inv_freq = (f32(1.0) / f32(10000.0) ** (np.arange(0, D, 2, dtype=f32) / f32(D))).astype(f32)
    ang = np.arange(N, dtype=f32)[:, None] * inv_freq[None, :]
    root = np.sqrt(np.sqrt(1.0 / D))
    cos = (np.cos(ang.astype(np.float64)) * root).reshape(C, P128, D // 2).transpose(1, 0, 2)
    sin = (np.sin(ang.astype(np.float64)) * root).reshape(C, P128, D // 2).transpose(1, 0, 2)
    cos2 = np.concatenate([cos, cos], axis=2).astype(f32)
    sin2 = np.concatenate([-sin, sin], axis=2).astype(f32)
    s = np.arange(P128)[:, None]
    t = np.arange(P128)[None, :]
    cmat = np.concatenate([s == t, s <= t, (s <= t).astype(f32) - (s < 64), s < 64, s >= 64], axis=1).astype(f32)
    bf16 = mybir.dt.np(BF16)
    cmask = np.stack([(s == t).astype(f32), np.where(t > s, f32(NEG), f32(0.0))], axis=1).astype(bf16)
    expert = (np.arange(E * F) // F).reshape(FT, P128)
    csel = np.zeros((P128, FT, P128), f32)
    for e in range(E):
        csel[e] = expert == e
        csel[E + e] = expert == e

    wffn = np.concatenate([wgu.reshape(P128, FT, KT2 * 2 * P128), wdn], axis=2)
    named = {"x_rows": x, "x_cols": x.T, "wqkv": wqkv.reshape(P128, KV, KT2 * QKV), "wo_in": wo.reshape(P128, H * HID),
             "wffn": wffn, "gate": gate, "rope_cos": cos2, "rope_sin": sin2, "cmat": cmat, "cmask": cmask,
             "csel": csel.reshape(P128, FT * P128)}
    nc = bacc.Bacc("TRN2", target_bir_lowering=False, num_devices=1)
    arrays, aps = {}, {}
    for name, a in named.items():
        a = np.ascontiguousarray(a)
        arrays["in_" + name] = a
        aps[name] = nc.dram_tensor("in_" + name, a.shape, mybir.dt.from_np(a.dtype), kind="ExternalInput").ap()
    out = nc.dram_tensor("out_0", (B, N, HID), F32, kind="ExternalOutput").ap()
    layer_kernel(nc, out=out, **aps)
    r = run_bass_kernel_spmd(nc, [arrays], core_ids=[0])
    return r.results[0]["out_0"]
```
